# Optimizing a Trainium2 kernel written in Bass

```python
import numpy as np
import jax
import jax.numpy as jnp

def _softmax(x, axis=-1):
    return jax.nn.softmax(x, axis=axis)

def _gelu(x):
    return jax.nn.gelu(x, approximate=True)

def _silu(x):
    return jax.nn.silu(x)

def _sigmoid(x):
    return jax.nn.sigmoid(x)

def _layernorm(x, axis=-1, eps=1e-05):
    m = jnp.mean(x, axis=axis, keepdims=True)
    v = jnp.var(x, axis=axis, keepdims=True)
    return (x - m) / jnp.sqrt(v + eps)

def _scatter_add(tgt, idx, src, axis=0):
    return tgt.at[idx].add(src)

def _segment_sum(src, seg, n):
    return jax.ops.segment_sum(src, seg, n)
kernel_name = 'mk_perceiver_d2_seqx_r8_faac02'

def setup_inputs(seed: int=0):
    np.random.seed(seed)
    _w = jnp.asarray

    def _rec_inputs():
        import jax
        import jax.numpy as jnp
        _rk = jax.random.key(seed)
        x = -0.0002928 + 1 * jax.random.normal(jax.random.fold_in(_rk, 1), (32, 64, 128), jnp.float32)
        _lenS = 64 - jax.random.randint(jax.random.fold_in(_rk, 7), (32,), 0, max(1, 64 // 4) + 1, jnp.int32)
        _lenS2 = 1601 - jax.random.randint(jax.random.fold_in(_rk, 8), (32,), 0, max(1, 1601 // 4) + 1, jnp.int32)
        _ctx_1024P = jax.random.normal(jax.random.fold_in(_rk, 11), (32, 16, 128), jnp.float32)
        _ctx_1024c = jax.random.dirichlet(jax.random.fold_in(_rk, 511), 0.3 * jnp.ones((16,), jnp.float32), (32, 1601))
        _ctx_1024t = jnp.einsum('bsk,bkd->bsd', _ctx_1024c, _ctx_1024P)
        _ctx_1024t = _ctx_1024t * jax.lax.rsqrt(jnp.mean(jnp.square(_ctx_1024t)) + 1e-12) * 0.953939
        ctx_1024 = -1.39393e-06 + 0.999914 * (_ctx_1024t + 0.3 * jax.random.normal(jax.random.fold_in(_rk, 611), (32, 1601, 128), jnp.float32))
        _validS = jnp.arange(64)[None, :] < _lenS[:, None]
        _validS2 = jnp.arange(1601)[None, :] < _lenS2[:, None]
        _causal = jnp.tril(jnp.ones((64, 64), dtype=bool))
        mask_BxS2_bf1 = jnp.ones((32, 1601), dtype=bool)
        return (x, ctx_1024, mask_BxS2_bf1)
    x, ctx_1024, mask_BxS2_bf1 = _rec_inputs()

    def _L0_xattn_setup():
        import jax, jax.numpy as jnp
        import numpy as np
        import math
        NHEAD = 16
        EPS = 1e-05

        def _layernorm(x, g, b):
            m = jnp.mean(x, axis=-1, keepdims=True)
            v = jnp.var(x, axis=-1, keepdims=True)
            return (x - m) / jnp.sqrt(v + EPS) * g + b

        def _split_heads(t, H):
            B, L, D = t.shape
            return t.reshape(B, L, H, D // H).transpose(0, 2, 1, 3)

        def _merge_heads(t):
            B, H, L, hd = t.shape
            return t.transpose(0, 2, 1, 3).reshape(B, L, H * hd)

        def _prob_sparse_self_attn(x, out_w, out_b):
            B, L, D = x.shape
            H = NHEAD
            q = _split_heads(x, H)
            k = q
            v = q
            scores = jnp.einsum('bhqd,bhkd->bhqk', q, k) * (1.0 / math.sqrt(D))
            u = max(1, int(math.ceil(math.log(L + 1))))
            _, idx = jax.lax.top_k(scores, u)
            bi = jnp.arange(B)[:, None, None, None]
            hi = jnp.arange(H)[None, :, None, None]
            li = jnp.arange(L)[None, None, :, None]
            mask = jnp.zeros(scores.shape, bool).at[bi, hi, li, idx].set(True)
            scores = jnp.where(mask, scores, -jnp.inf)
            attn = jax.nn.softmax(scores, axis=-1)
            out = _merge_heads(jnp.einsum('bhqk,bhkd->bhqd', attn, v))
            return out @ out_w.T + out_b

        def _mha_cross(x, mem, in_w, in_b, out_w, out_b):
            B, L, D = x.shape
            H = NHEAD
            hd = D // H
            wq, wk, wv = (in_w[:D], in_w[D:2 * D], in_w[2 * D:])
            bq, bk, bv = (in_b[:D], in_b[D:2 * D], in_b[2 * D:])
            q = _split_heads(x @ wq.T + bq, H)
            k = _split_heads(mem @ wk.T + bk, H)
            v = _split_heads(mem @ wv.T + bv, H)
            scores = jnp.einsum('bhqd,bhkd->bhqk', q, k) * (1.0 / math.sqrt(hd))
            attn = jax.nn.softmax(scores, axis=-1)
            out = _merge_heads(jnp.einsum('bhqk,bhkd->bhqd', attn, v))
            return out @ out_w.T + out_b
        key = jax.random.key(seed)
        ks = jax.random.split(key, 16)
        B, L, S, D, F = (2, 256, 256, 128, 512)
        s = 0.02
        inp = {'x': jax.random.normal(ks[0], (B, L, D), jnp.float32), 'memory': jax.random.normal(ks[1], (B, S, D), jnp.float32), 'self_out_w': jax.random.normal(ks[2], (D, D), jnp.float32) * s, 'self_out_b': jnp.zeros((D,), jnp.float32), 'cross_in_w': jax.random.normal(ks[3], (3 * D, D), jnp.float32) * s, 'cross_in_b': jnp.zeros((3 * D,), jnp.float32), 'cross_out_w': jax.random.normal(ks[4], (D, D), jnp.float32) * s, 'cross_out_b': jnp.zeros((D,), jnp.float32), 'ln1_g': jnp.ones((D,), jnp.float32), 'ln1_b': jnp.zeros((D,), jnp.float32), 'ln2_g': jnp.ones((D,), jnp.float32), 'ln2_b': jnp.zeros((D,), jnp.float32), 'ln3_g': jnp.ones((D,), jnp.float32), 'ln3_b': jnp.zeros((D,), jnp.float32), 'ffn_w1': jax.random.normal(ks[5], (F, D), jnp.float32) * s, 'ffn_b1': jnp.zeros((F,), jnp.float32), 'ffn_w2': jax.random.normal(ks[6], (D, F), jnp.float32) * s, 'ffn_b2': jnp.zeros((D,), jnp.float32)}
        return inp
    _L0_xattn_all = _L0_xattn_setup()
    _L0_xattn_in = {k: v for k, v in _L0_xattn_all.items() if k in ('self_out_w', 'self_out_b', 'cross_in_w', 'cross_in_b', 'cross_out_w', 'cross_out_b', 'ln1_g', 'ln1_b', 'ln2_g', 'ln2_b', 'ln3_g', 'ln3_b', 'ffn_w1', 'ffn_b1', 'ffn_w2', 'ffn_b2')}
    del _L0_xattn_all

    def _L0_attn_setup():
        import jax, jax.numpy as jnp
        import numpy as np
        B, N, D = (4, 256, 128)
        H = 8
        DK = D // H
        DV = D // H
        DF = 2 * DK
        CHUNK = 64
        RMS_EPS = 1e-05

        def _hedgehog(x, w, b):
            y = jnp.einsum('bhnd,ed->bhne', x, w) + b
            return jnp.concatenate([jnp.exp(y), jnp.exp(-y)], axis=-1)

        def _fused_chunk_linear_attn(q, k, v):
            b, h, n, df = q.shape
            dv = v.shape[-1]
            nc = n // CHUNK

            def to_chunks(t):
                d = t.shape[-1]
                return t.reshape(b, h, nc, CHUNK, d).transpose(2, 0, 1, 3, 4)
            qc, kc, vc = (to_chunks(q), to_chunks(k), to_chunks(v))
            mask = jnp.tril(jnp.ones((CHUNK, CHUNK), dtype=bool))

            def step(S, inp):
                qi, ki, vi = inp
                attn = jnp.einsum('bhcd,bhed->bhce', qi, ki)
                attn = jnp.where(mask, attn, 0.0)
                intra = jnp.einsum('bhce,bhev->bhcv', attn, vi)
                inter = jnp.einsum('bhcd,bhdv->bhcv', qi, S)
                S = S + jnp.einsum('bhcd,bhcv->bhdv', ki, vi)
                return (S, intra + inter)
            S0 = jnp.zeros((b, h, df, dv), dtype=q.dtype)
            _, oc = jax.lax.scan(step, S0, (qc, kc, vc))
            return oc.transpose(1, 2, 0, 3, 4).reshape(b, h, n, dv)
        key = jax.random.key(seed)
        ks = jax.random.split(key, 10)
        s = D ** (-0.5)
        x = jax.random.normal(ks[0], (B, N, D), dtype=jnp.float32)
        Wq = jax.random.normal(ks[1], (D, D), dtype=jnp.float32) * s
        Wk = jax.random.normal(ks[2], (D, D), dtype=jnp.float32) * s
        Wv = jax.random.normal(ks[3], (D, D), dtype=jnp.float32) * s
        Wo = jax.random.normal(ks[4], (D, D), dtype=jnp.float32) * s
        eye = jnp.eye(DK, dtype=jnp.float32)
        fmq_w = eye + 0.02 * jax.random.normal(ks[5], (DK, DK), dtype=jnp.float32)
        fmq_b = 0.02 * jax.random.normal(ks[6], (DK,), dtype=jnp.float32)
        fmk_w = eye + 0.02 * jax.random.normal(ks[7], (DK, DK), dtype=jnp.float32)
        fmk_b = 0.02 * jax.random.normal(ks[8], (DK,), dtype=jnp.float32)
        rms_w = 1.0 + 0.1 * jax.random.normal(ks[9], (DV,), dtype=jnp.float32)
        return {'x': x, 'Wq': Wq, 'Wk': Wk, 'Wv': Wv, 'Wo': Wo, 'fmq_w': fmq_w, 'fmq_b': fmq_b, 'fmk_w': fmk_w, 'fmk_b': fmk_b, 'rms_w': rms_w}
    _L0_attn_all = _L0_attn_setup()
    _L0_attn_in = {k: v for k, v in _L0_attn_all.items() if k in ('Wq', 'Wk', 'Wv', 'Wo', 'fmq_w', 'fmq_b', 'fmk_w', 'fmk_b', 'rms_w')}
    del _L0_attn_all

    def _L0_ffn_setup():
        import jax, jax.numpy as jnp
        import numpy as np
        B, N, E = (8, 256, 128)
        NUM_EXPERTS = 8
        HIDDEN = 192
        TOP_K = 2
        key = jax.random.key(seed)
        ks = jax.random.split(key, 7)
        s = 0.02
        return {'x': jax.random.normal(ks[0], (B, N, E), dtype=jnp.float32), 'Wr': jax.random.normal(ks[1], (E, NUM_EXPERTS), dtype=jnp.float32) * s, 'br': jnp.zeros((NUM_EXPERTS,), dtype=jnp.float32), 'W1': jax.random.normal(ks[2], (NUM_EXPERTS, E, HIDDEN), dtype=jnp.float32) * s, 'b1': jnp.zeros((NUM_EXPERTS, HIDDEN), dtype=jnp.float32), 'W2': jax.random.normal(ks[3], (NUM_EXPERTS, HIDDEN, E), dtype=jnp.float32) * s, 'b2': jnp.zeros((NUM_EXPERTS, E), dtype=jnp.float32)}
    _L0_ffn_all = _L0_ffn_setup()
    _L0_ffn_in = {k: v for k, v in _L0_ffn_all.items() if k in ('Wr', 'br', 'W1', 'b1', 'W2', 'b2')}
    del _L0_ffn_all

    def _L1_xattn_setup():
        import jax, jax.numpy as jnp
        import numpy as np
        HEADS = 16
        DIM_HEAD = 64
        SCALE = DIM_HEAD ** (-0.5)
        key = jax.random.key(seed)
        ks = jax.random.split(key, 6)
        B, Nq, Nkv, D = (4, 256, 128, 128)
        inner = HEADS * DIM_HEAD
        return {'x': jax.random.normal(ks[0], (B, Nq, D), dtype=jnp.float32), 'context': jax.random.normal(ks[1], (B, Nkv, D), dtype=jnp.float32), 'mask': jnp.ones((B, Nkv), dtype=bool), 'Wq': jax.random.normal(ks[2], (inner, D), dtype=jnp.float32) * D ** (-0.5), 'Wkv': jax.random.normal(ks[3], (2 * inner, D), dtype=jnp.float32) * D ** (-0.5), 'Wout': jax.random.normal(ks[4], (D, inner), dtype=jnp.float32) * inner ** (-0.5), 'b_out': jnp.zeros((D,), dtype=jnp.float32)}
    _L1_xattn_all = _L1_xattn_setup()
    _L1_xattn_in = {k: v for k, v in _L1_xattn_all.items() if k in ('Wq', 'Wkv', 'Wout', 'b_out')}
    del _L1_xattn_all

    def _L1_attn_setup():
        import jax, jax.numpy as jnp
        import numpy as np
        B, T, E, H = (1, 256, 128, 16)
        HD = E // H
        key = jax.random.key(seed)
        ks = jax.random.split(key, 8)
        s = 0.02
        mk = lambda k, sh: jax.random.normal(k, sh, jnp.float32) * s
        return {'x': jax.random.normal(ks[0], (B, T, E), jnp.float32), 'wq': mk(ks[1], (E, E)), 'bq': jnp.zeros((E,), jnp.float32), 'wk': mk(ks[2], (E, E)), 'bk': jnp.zeros((E,), jnp.float32), 'wv': mk(ks[3], (E, E)), 'bv': jnp.zeros((E,), jnp.float32), 'wg': mk(ks[4], (E, E)), 'bg': jnp.zeros((E,), jnp.float32), 'wo': mk(ks[5], (E, E)), 'bo': jnp.zeros((E,), jnp.float32), 'wd': mk(ks[6], (H, E)), 'bd': jnp.zeros((H,), jnp.float32), 'gamma': jnp.ones((E,), jnp.float32), 'beta': jnp.zeros((E,), jnp.float32)}
    _L1_attn_all = _L1_attn_setup()
    _L1_attn_in = {k: v for k, v in _L1_attn_all.items() if k in ('wq', 'bq', 'wk', 'bk', 'wv', 'bv', 'wg', 'bg', 'wo', 'bo', 'wd', 'bd', 'gamma', 'beta')}
    del _L1_attn_all

    def _L1_ffn_setup():
        import jax, jax.numpy as jnp
        import numpy as np
        D_MODEL = 128
        D_FF = 512
        N_EXPERTS = 8
        TOP_K = 2
        B, S = (2, 256)
        key = jax.random.key(seed)
        ks = jax.random.split(key, 9)
        s_in = 1.0 / np.sqrt(D_MODEL)
        s_ff = 1.0 / np.sqrt(D_FF)
        return {'x': jax.random.normal(ks[0], (B, S, D_MODEL), dtype=jnp.float32), 'Wr': jax.random.normal(ks[1], (D_MODEL, N_EXPERTS), dtype=jnp.float32) * s_in, 'br': jnp.zeros((N_EXPERTS,), dtype=jnp.float32), 'W1': jax.random.normal(ks[2], (N_EXPERTS, D_MODEL, D_FF), dtype=jnp.float32) * s_in, 'b1': jnp.zeros((N_EXPERTS, D_FF), dtype=jnp.float32), 'W2': jax.random.normal(ks[3], (N_EXPERTS, D_MODEL, D_FF), dtype=jnp.float32) * s_in, 'b2': jnp.zeros((N_EXPERTS, D_FF), dtype=jnp.float32), 'W3': jax.random.normal(ks[4], (N_EXPERTS, D_FF, D_MODEL), dtype=jnp.float32) * s_ff, 'b3': jnp.zeros((N_EXPERTS, D_MODEL), dtype=jnp.float32)}
    _L1_ffn_all = _L1_ffn_setup()
    _L1_ffn_in = {k: v for k, v in _L1_ffn_all.items() if k in ('Wr', 'br', 'W1', 'b1', 'W2', 'b2', 'W3', 'b3')}
    del _L1_ffn_all
    return {'x': x, 'ctx_1024': ctx_1024, 'mask_BxS2_bf1': mask_BxS2_bf1, 'L0_xattn_self_out_w': _L0_xattn_in['self_out_w'], 'L0_xattn_self_out_b': _L0_xattn_in['self_out_b'], 'L0_xattn_cross_in_w': _L0_xattn_in['cross_in_w'], 'L0_xattn_cross_in_b': _L0_xattn_in['cross_in_b'], 'L0_xattn_cross_out_w': _L0_xattn_in['cross_out_w'], 'L0_xattn_cross_out_b': _L0_xattn_in['cross_out_b'], 'L0_xattn_ln1_g': _L0_xattn_in['ln1_g'], 'L0_xattn_ln1_b': _L0_xattn_in['ln1_b'], 'L0_xattn_ln2_g': _L0_xattn_in['ln2_g'], 'L0_xattn_ln2_b': _L0_xattn_in['ln2_b'], 'L0_xattn_ln3_g': _L0_xattn_in['ln3_g'], 'L0_xattn_ln3_b': _L0_xattn_in['ln3_b'], 'L0_xattn_ffn_w1': _L0_xattn_in['ffn_w1'], 'L0_xattn_ffn_b1': _L0_xattn_in['ffn_b1'], 'L0_xattn_ffn_w2': _L0_xattn_in['ffn_w2'], 'L0_xattn_ffn_b2': _L0_xattn_in['ffn_b2'], 'L0_attn_Wq': _L0_attn_in['Wq'], 'L0_attn_Wk': _L0_attn_in['Wk'], 'L0_attn_Wv': _L0_attn_in['Wv'], 'L0_attn_Wo': _L0_attn_in['Wo'], 'L0_attn_fmq_w': _L0_attn_in['fmq_w'], 'L0_attn_fmq_b': _L0_attn_in['fmq_b'], 'L0_attn_fmk_w': _L0_attn_in['fmk_w'], 'L0_attn_fmk_b': _L0_attn_in['fmk_b'], 'L0_attn_rms_w': _L0_attn_in['rms_w'], 'L0_ffn_Wr': _L0_ffn_in['Wr'], 'L0_ffn_br': _L0_ffn_in['br'], 'L0_ffn_W1': _L0_ffn_in['W1'], 'L0_ffn_b1': _L0_ffn_in['b1'], 'L0_ffn_W2': _L0_ffn_in['W2'], 'L0_ffn_b2': _L0_ffn_in['b2'], 'L1_xattn_Wq': _L1_xattn_in['Wq'], 'L1_xattn_Wkv': _L1_xattn_in['Wkv'], 'L1_xattn_Wout': _L1_xattn_in['Wout'], 'L1_xattn_b_out': _L1_xattn_in['b_out'], 'L1_attn_wq': _L1_attn_in['wq'], 'L1_attn_bq': _L1_attn_in['bq'], 'L1_attn_wk': _L1_attn_in['wk'], 'L1_attn_bk': _L1_attn_in['bk'], 'L1_attn_wv': _L1_attn_in['wv'], 'L1_attn_bv': _L1_attn_in['bv'], 'L1_attn_wg': _L1_attn_in['wg'], 'L1_attn_bg': _L1_attn_in['bg'], 'L1_attn_wo': _L1_attn_in['wo'], 'L1_attn_bo': _L1_attn_in['bo'], 'L1_attn_wd': _L1_attn_in['wd'], 'L1_attn_bd': _L1_attn_in['bd'], 'L1_attn_gamma': _L1_attn_in['gamma'], 'L1_attn_beta': _L1_attn_in['beta'], 'L1_ffn_Wr': _L1_ffn_in['Wr'], 'L1_ffn_br': _L1_ffn_in['br'], 'L1_ffn_W1': _L1_ffn_in['W1'], 'L1_ffn_b1': _L1_ffn_in['b1'], 'L1_ffn_W2': _L1_ffn_in['W2'], 'L1_ffn_b2': _L1_ffn_in['b2'], 'L1_ffn_W3': _L1_ffn_in['W3'], 'L1_ffn_b3': _L1_ffn_in['b3']}

def reference(x, ctx_1024, mask_BxS2_bf1, L0_xattn_self_out_w, L0_xattn_self_out_b, L0_xattn_cross_in_w, L0_xattn_cross_in_b, L0_xattn_cross_out_w, L0_xattn_cross_out_b, L0_xattn_ln1_g, L0_xattn_ln1_b, L0_xattn_ln2_g, L0_xattn_ln2_b, L0_xattn_ln3_g, L0_xattn_ln3_b, L0_xattn_ffn_w1, L0_xattn_ffn_b1, L0_xattn_ffn_w2, L0_xattn_ffn_b2, L0_attn_Wq, L0_attn_Wk, L0_attn_Wv, L0_attn_Wo, L0_attn_fmq_w, L0_attn_fmq_b, L0_attn_fmk_w, L0_attn_fmk_b, L0_attn_rms_w, L0_ffn_Wr, L0_ffn_br, L0_ffn_W1, L0_ffn_b1, L0_ffn_W2, L0_ffn_b2, L1_xattn_Wq, L1_xattn_Wkv, L1_xattn_Wout, L1_xattn_b_out, L1_attn_wq, L1_attn_bq, L1_attn_wk, L1_attn_bk, L1_attn_wv, L1_attn_bv, L1_attn_wg, L1_attn_bg, L1_attn_wo, L1_attn_bo, L1_attn_wd, L1_attn_bd, L1_attn_gamma, L1_attn_beta, L1_ffn_Wr, L1_ffn_br, L1_ffn_W1, L1_ffn_b1, L1_ffn_W2, L1_ffn_b2, L1_ffn_W3, L1_ffn_b3):
    import jax
    import jax.numpy as jnp

    def _L0_xattn_ref(x, memory, self_out_w, self_out_b, cross_in_w, cross_in_b, cross_out_w, cross_out_b, ln1_g, ln1_b, ln2_g, ln2_b, ln3_g, ln3_b, ffn_w1, ffn_b1, ffn_w2, ffn_b2):
        import jax, jax.numpy as jnp
        import numpy as np
        import math
        NHEAD = 16
        EPS = 1e-05

        def _layernorm(x, g, b):
            m = jnp.mean(x, axis=-1, keepdims=True)
            v = jnp.var(x, axis=-1, keepdims=True)
            return (x - m) / jnp.sqrt(v + EPS) * g + b

        def _split_heads(t, H):
            B, L, D = t.shape
            return t.reshape(B, L, H, D // H).transpose(0, 2, 1, 3)

        def _merge_heads(t):
            B, H, L, hd = t.shape
            return t.transpose(0, 2, 1, 3).reshape(B, L, H * hd)

        def _prob_sparse_self_attn(x, out_w, out_b):
            B, L, D = x.shape
            H = NHEAD
            q = _split_heads(x, H)
            k = q
            v = q
            scores = jnp.einsum('bhqd,bhkd->bhqk', q, k) * (1.0 / math.sqrt(D))
            u = max(1, int(math.ceil(math.log(L + 1))))
            _, idx = jax.lax.top_k(scores, u)
            bi = jnp.arange(B)[:, None, None, None]
            hi = jnp.arange(H)[None, :, None, None]
            li = jnp.arange(L)[None, None, :, None]
            mask = jnp.zeros(scores.shape, bool).at[bi, hi, li, idx].set(True)
            scores = jnp.where(mask, scores, -jnp.inf)
            attn = jax.nn.softmax(scores, axis=-1)
            out = _merge_heads(jnp.einsum('bhqk,bhkd->bhqd', attn, v))
            return out @ out_w.T + out_b

        def _mha_cross(x, mem, in_w, in_b, out_w, out_b):
            B, L, D = x.shape
            H = NHEAD
            hd = D // H
            wq, wk, wv = (in_w[:D], in_w[D:2 * D], in_w[2 * D:])
            bq, bk, bv = (in_b[:D], in_b[D:2 * D], in_b[2 * D:])
            q = _split_heads(x @ wq.T + bq, H)
            k = _split_heads(mem @ wk.T + bk, H)
            v = _split_heads(mem @ wv.T + bv, H)
            scores = jnp.einsum('bhqd,bhkd->bhqk', q, k) * (1.0 / math.sqrt(hd))
            attn = jax.nn.softmax(scores, axis=-1)
            out = _merge_heads(jnp.einsum('bhqk,bhkd->bhqd', attn, v))
            return out @ out_w.T + out_b
        x_self = _prob_sparse_self_attn(x, self_out_w, self_out_b)
        x = _layernorm(x + x_self, ln1_g, ln1_b)
        x_cross = _mha_cross(x, memory, cross_in_w, cross_in_b, cross_out_w, cross_out_b)
        x = _layernorm(x + x_cross, ln2_g, ln2_b)
        h = jax.nn.gelu(x @ ffn_w1.T + ffn_b1, approximate=False)
        x_ffn = h @ ffn_w2.T + ffn_b2
        x = _layernorm(x + x_ffn, ln3_g, ln3_b)
        return x

    def _L0_attn_ref(x, Wq, Wk, Wv, Wo, fmq_w, fmq_b, fmk_w, fmk_b, rms_w):
        import jax, jax.numpy as jnp
        import numpy as np
        B, N, D = (4, 256, 128)
        H = 8
        DK = D // H
        DV = D // H
        DF = 2 * DK
        CHUNK = 64
        RMS_EPS = 1e-05

        def _hedgehog(x, w, b):
            y = jnp.einsum('bhnd,ed->bhne', x, w) + b
            return jnp.concatenate([jnp.exp(y), jnp.exp(-y)], axis=-1)

        def _fused_chunk_linear_attn(q, k, v):
            b, h, n, df = q.shape
            dv = v.shape[-1]
            nc = n // CHUNK

            def to_chunks(t):
                d = t.shape[-1]
                return t.reshape(b, h, nc, CHUNK, d).transpose(2, 0, 1, 3, 4)
            qc, kc, vc = (to_chunks(q), to_chunks(k), to_chunks(v))
            mask = jnp.tril(jnp.ones((CHUNK, CHUNK), dtype=bool))

            def step(S, inp):
                qi, ki, vi = inp
                attn = jnp.einsum('bhcd,bhed->bhce', qi, ki)
                attn = jnp.where(mask, attn, 0.0)
                intra = jnp.einsum('bhce,bhev->bhcv', attn, vi)
                inter = jnp.einsum('bhcd,bhdv->bhcv', qi, S)
                S = S + jnp.einsum('bhcd,bhcv->bhdv', ki, vi)
                return (S, intra + inter)
            S0 = jnp.zeros((b, h, df, dv), dtype=q.dtype)
            _, oc = jax.lax.scan(step, S0, (qc, kc, vc))
            return oc.transpose(1, 2, 0, 3, 4).reshape(b, h, n, dv)
        b, n, d = x.shape
        split = lambda t: t.reshape(b, n, H, -1).transpose(0, 2, 1, 3)
        q = split(x @ Wq.T)
        k = split(x @ Wk.T)
        v = split(x @ Wv.T)
        q = _hedgehog(q, fmq_w, fmq_b)
        k = _hedgehog(k, fmk_w, fmk_b)
        scale = q.shape[-1] ** (-0.5)
        o = _fused_chunk_linear_attn(q * scale, k, v)
        o = o * jax.lax.rsqrt(jnp.mean(o * o, axis=-1, keepdims=True) + RMS_EPS) * rms_w
        o = o.transpose(0, 2, 1, 3).reshape(b, n, H * DV)
        return o @ Wo.T

    def _L0_ffn_ref(x, Wr, br, W1, b1, W2, b2):
        import jax, jax.numpy as jnp
        import numpy as np
        B, N, E = (8, 256, 128)
        NUM_EXPERTS = 8
        HIDDEN = 192
        TOP_K = 2
        b, n, e = x.shape
        T = b * n
        logits = jnp.einsum('bne,ec->bnc', x, Wr) + br
        probs = jax.nn.softmax(logits, axis=-1)
        topk_probs, topk_idx = jax.lax.top_k(probs, TOP_K)
        flat_x = x.reshape(T, e)
        flat_w = topk_probs.reshape(T, TOP_K)
        flat_idx = topk_idx.reshape(T, TOP_K)
        onehot = jax.nn.one_hot(flat_idx, NUM_EXPERTS, dtype=flat_w.dtype)
        combine = jnp.einsum('tk,tke->te', flat_w, onehot)
        out = jnp.zeros_like(flat_x)
        for ei in range(NUM_EXPERTS):
            h = jax.nn.gelu(flat_x @ W1[ei] + b1[ei], approximate=False)
            y = h @ W2[ei] + b2[ei]
            out = out + combine[:, ei:ei + 1] * y
        return out.reshape(b, n, e)

    def _L1_xattn_ref(x, context, mask, Wq, Wkv, Wout, b_out):
        import jax, jax.numpy as jnp
        import numpy as np
        HEADS = 16
        DIM_HEAD = 64
        SCALE = DIM_HEAD ** (-0.5)
        B, Nq, _ = x.shape
        Nkv = context.shape[1]
        q = x @ Wq.T
        kv = context @ Wkv.T
        k, v = jnp.split(kv, 2, axis=-1)
        q = q.reshape(B, Nq, HEADS, DIM_HEAD).transpose(0, 2, 1, 3)
        k = k.reshape(B, Nkv, HEADS, DIM_HEAD).transpose(0, 2, 1, 3)
        v = v.reshape(B, Nkv, HEADS, DIM_HEAD).transpose(0, 2, 1, 3)
        sim = jnp.einsum('bhid,bhjd->bhij', q, k) * SCALE
        max_neg = -jnp.finfo(sim.dtype).max
        sim = jnp.where(mask[:, None, None, :], sim, max_neg)
        attn = jax.nn.softmax(sim, axis=-1)
        out = jnp.einsum('bhij,bhjd->bhid', attn, v)
        out = out.transpose(0, 2, 1, 3).reshape(B, Nq, HEADS * DIM_HEAD)
        return out @ Wout.T + b_out

    def _L1_attn_ref(x, wq, bq, wk, bk, wv, bv, wg, bg, wo, bo, wd, bd, gamma, beta):
        import jax, jax.numpy as jnp
        import numpy as np
        B, T, E, H = (1, 256, 128, 16)
        HD = E // H
        Bx, Tx, Ex = x.shape
        scale = jnp.sqrt(jnp.asarray(HD, jnp.float32))

        def proj(w, b):
            return (x @ w.T + b).reshape(Bx, Tx, H, HD).transpose(0, 2, 1, 3)
        Q, K, V = (proj(wq, bq), proj(wk, bk), proj(wv, bv))
        inv_freq = 1.0 / 10000.0 ** (jnp.arange(0, HD, 2, dtype=jnp.float32) / HD)
        freqs = jnp.arange(Tx, dtype=jnp.float32)[:, None] * inv_freq[None, :]
        emb = jnp.concatenate([freqs, freqs], axis=-1)
        cos, sin = (jnp.cos(emb), jnp.sin(emb))

        def rope(t):
            x1, x2 = (t[..., ::2], t[..., 1::2])
            t_rot = jnp.stack([-x2, x1], axis=-1).reshape(t.shape)
            return t * cos + t_rot * sin
        Q, K = (rope(Q), rope(K))
        scores = jnp.einsum('bhqd,bhkd->bhqk', Q, K) / scale
        pd = jax.nn.sigmoid(x.mean(axis=1) @ wd.T + bd)
        log_decay = jnp.log(1.0 - jnp.exp2(-5.0 - 8.0 * pd))
        idx = jnp.arange(Tx)
        pos_diff = jnp.clip(idx[None, :] - idx[:, None], 0, None).astype(jnp.float32)
        scores = scores + pos_diff[None, None] * log_decay[:, :, None, None]
        attn = jax.nn.softmax(scores, axis=-1)
        out = jnp.einsum('bhqk,bhkd->bhqd', attn, V).transpose(0, 2, 1, 3).reshape(Bx, Tx, Ex)
        og = out.reshape(Bx, Tx, H, HD)
        mu = og.mean(axis=(1, 3), keepdims=True)
        var = ((og - mu) ** 2).mean(axis=(1, 3), keepdims=True)
        on = ((og - mu) / jnp.sqrt(var + 1e-05)).reshape(Bx, Tx, Ex) * gamma + beta
        gate = jax.nn.silu(x @ wg.T + bg)
        return gate * on @ wo.T + bo

    def _L1_ffn_ref(x, Wr, br, W1, b1, W2, b2, W3, b3):
        import jax, jax.numpy as jnp
        import numpy as np
        D_MODEL = 128
        D_FF = 512
        N_EXPERTS = 8
        TOP_K = 2
        B, S = (2, 256)
        logits = jnp.einsum('bsd,de->bse', x, Wr) + br
        top_vals, top_idx = jax.lax.top_k(logits, TOP_K)
        top_w = jax.nn.softmax(top_vals, axis=-1)
        comb = jnp.sum(jax.nn.one_hot(top_idx, N_EXPERTS, dtype=x.dtype) * top_w[..., None], axis=-2)
        out = jnp.zeros_like(x)
        for e in range(N_EXPERTS):
            gate = jax.nn.silu(jnp.einsum('bsd,df->bsf', x, W1[e]) + b1[e])
            h = (jnp.einsum('bsd,df->bsf', x, W2[e]) + b2[e]) * gate
            y = jnp.einsum('bsf,fd->bsd', h, W3[e]) + b3[e]
            out = out + comb[..., e:e + 1] * y
        return out
    x = x + _L0_xattn_ref(_layernorm(x, axis=-1), ctx_1024, L0_xattn_self_out_w, L0_xattn_self_out_b, L0_xattn_cross_in_w, L0_xattn_cross_in_b, L0_xattn_cross_out_w, L0_xattn_cross_out_b, L0_xattn_ln1_g, L0_xattn_ln1_b, L0_xattn_ln2_g, L0_xattn_ln2_b, L0_xattn_ln3_g, L0_xattn_ln3_b, L0_xattn_ffn_w1, L0_xattn_ffn_b1, L0_xattn_ffn_w2, L0_xattn_ffn_b2)
    x = x + _L0_attn_ref(_layernorm(x, axis=-1), L0_attn_Wq, L0_attn_Wk, L0_attn_Wv, L0_attn_Wo, L0_attn_fmq_w, L0_attn_fmq_b, L0_attn_fmk_w, L0_attn_fmk_b, L0_attn_rms_w)
    x = x + _L0_ffn_ref(_layernorm(x, axis=-1), L0_ffn_Wr, L0_ffn_br, L0_ffn_W1, L0_ffn_b1, L0_ffn_W2, L0_ffn_b2)
    x = x + _L1_xattn_ref(_layernorm(x, axis=-1), ctx_1024, mask_BxS2_bf1, L1_xattn_Wq, L1_xattn_Wkv, L1_xattn_Wout, L1_xattn_b_out)
    x = x + _L1_attn_ref(_layernorm(x, axis=-1), L1_attn_wq, L1_attn_bq, L1_attn_wk, L1_attn_bk, L1_attn_wv, L1_attn_bv, L1_attn_wg, L1_attn_bg, L1_attn_wo, L1_attn_bo, L1_attn_wd, L1_attn_bd, L1_attn_gamma, L1_attn_beta)
    x = x + _L1_ffn_ref(_layernorm(x, axis=-1), L1_ffn_Wr, L1_ffn_br, L1_ffn_W1, L1_ffn_b1, L1_ffn_W2, L1_ffn_b2, L1_ffn_W3, L1_ffn_b3)
    return x

_drawn_inputs = setup_inputs


def setup_inputs(seed=0):
    import zlib

    import numpy as np

    out = dict(_drawn_inputs(seed))
    spreads = {'L0_xattn_self_out_b': (0.0, 0.1),
     'L0_xattn_cross_in_b': (0.0, 0.1),
     'L0_xattn_cross_out_b': (0.0, 0.1),
     'L0_xattn_ln1_g': (1.0, 0.2),
     'L0_xattn_ln1_b': (0.0, 0.1),
     'L0_xattn_ln2_g': (1.0, 0.2),
     'L0_xattn_ln2_b': (0.0, 0.1),
     'L0_xattn_ln3_g': (1.0, 0.2),
     'L0_xattn_ln3_b': (0.0, 0.1),
     'L0_xattn_ffn_b1': (0.0, 0.1),
     'L0_xattn_ffn_b2': (0.0, 0.1),
     'L0_ffn_br': (0.0, 0.448),
     'L0_ffn_b1': (0.0, 0.8),
     'L0_ffn_b2': (0.0, 0.48),
     'L1_xattn_b_out': (0.0, 0.1),
     'L1_attn_bq': (0.0, 0.8),
     'L1_attn_bk': (0.0, 2.0),
     'L1_attn_bv': (0.0, 0.429),
     'L1_attn_bg': (0.0, 0.554),
     'L1_attn_bo': (0.0, 0.1),
     'L1_attn_bd': (0.0, 2.0),
     'L1_attn_gamma': (1.0, 0.6),
     'L1_attn_beta': (0.0, 0.8),
     'L1_ffn_br': (0.0, 0.1),
     'L1_ffn_b1': (0.0, 0.403),
     'L1_ffn_b2': (0.0, 0.432),
     'L1_ffn_b3': (0.0, 0.277)}
    factors = {'L0_attn_fmq_b': 8.0,
     'L0_attn_fmk_b': 7.307,
     'L0_ffn_Wr': 3.74,
     'L0_ffn_W1': 6.697,
     'L0_ffn_W2': 5.092,
     'L1_attn_wq': 8.0,
     'L1_attn_wk': 8.0,
     'L1_attn_wv': 3.418,
     'L1_attn_wg': 3.138,
     'L1_attn_wd': 64.0}
    for name, (base, spread) in spreads.items():
        noise = np.random.default_rng([zlib.crc32(name.encode()), seed]).standard_normal(out[name].shape)
        drawn = base * np.exp(spread * noise) if base else spread * noise
        out[name] = jnp.asarray(drawn.astype(out[name].dtype))
    for name, factor in factors.items():
        out[name] = (out[name] * factor).astype(out[name].dtype)
    return out
```

```python
from contextlib import ExitStack

import numpy as np

import concourse.bass as bass
from concourse import mybir

P = 128
B, L, D = 32, 64, 128
S = 1601
PAIRS = B // 2
G = 4
GROUPS = PAIRS // G
H = 16
HD = D // H
HP = H // 2
LH = 8
LD = D // LH
XD = 64
E = 8
F0 = 512
F1 = 192
F2 = 512
U1 = E * F1 // P
FT = F2 // P
TOPU = 5
PAD = 8 - TOPU
EPS = 1e-5
BIG = 3.0e38
GONE = -1.0e30
LN2 = float(np.log(2.0))
KT = -(-S // P)
KL = S - (KT - 1) * P

F32 = mybir.dt.float32
BF16 = mybir.dt.bfloat16
U8 = mybir.dt.uint8
ALU = mybir.AluOpType
ACT = mybir.ActivationFunctionType
AX = mybir.AxisListType.X

STAGES = 10



def layout(items):
    at, n = {}, 0
    for name, w in items:
        at[name] = (n, w)
        n += w
    return at, n


W_ITEMS = [("self_out", D), ("c_wq", D), ("c_wk", D), ("c_wv", D), ("c_out", D), ("ffn1", F0), ("ffn2", F0),
           ("l_wq", D), ("l_wk", D), ("l_wv", D), ("l_wo", D), ("l_fq", D), ("l_fk", D),
           ("r1", E), ("r2", E), ("m1_b1", U1), ("m1_b2", D), ("m2_b1", E * FT), ("m2_b2", E * FT), ("m2_b3", D),
           ("a_wq", D), ("a_wqT", D), ("a_wk", D), ("a_wkT", D), ("a_wv", D), ("a_wg", D), ("a_wo", D), ("a_wd", H),
           ("c_bq", 1), ("c_bv", 1), ("ffn_b1", F0 // P), ("l_bq", 1), ("l_bk", 1), ("a_bq", 1), ("a_bk", 1)]
W_AT, W_N = layout(W_ITEMS)
R_ITEMS = [("self_out_b", D), ("c_out_b", D), ("ln1_g", D), ("ln1_b", D), ("ln2_g", D), ("ln2_b", D),
           ("ln3_g", D), ("ln3_b", D), ("ffn_b2", D), ("rms", D), ("x_b", D), ("a_bv", D), ("a_bg", D),
           ("a_bo", D), ("a_g", D), ("a_b", D), ("br1", E), ("br2", E), ("a_bd", H)]
R_AT, R_N = layout(R_ITEMS)
C_ITEMS = [("ident", P), ("head8", H), ("head16", LH), ("stack", L), ("half", 2), ("avg64", P), ("avg512", P),
           ("causal", L), ("rot", P), ("cos", L), ("sin", L), ("dist", L)]
C_AT, C_N = layout(C_ITEMS)


def constants():
    p = np.arange(P)
    t = {}
    t["ident"] = np.eye(P)
    t["head8"] = (p[:, None] // HD == np.arange(H)[None])
    t["head16"] = (p[:, None] // LD == np.arange(LH)[None])
    t["stack"] = (p[:, None] % L == np.arange(L)[None])
    t["half"] = (p[:, None] // L == np.arange(2)[None])
    same = (p[:, None] // L == p[None] // L)
    t["avg64"] = same / L
    t["avg512"] = same / (L * HD)
    t["causal"] = (p[:, None] % L <= np.arange(L)[None]) * (2 * LD) ** -0.5
    rot = np.zeros((P, P))
    rot[p[1::2], p[0::2]] = -1.0
    rot[p[0::2], p[1::2]] = 1.0
    t["rot"] = rot
    inv = (1.0 / np.float32(10000.0) ** (np.arange(0, HD, 2, dtype=np.float32) / np.float32(HD))).astype(np.float32)
    fr = np.arange(L, dtype=np.float32)[:, None] * inv[None]
    emb = np.concatenate([fr, fr], -1)
    t["cos"] = np.cos(emb).T[p % HD]
    t["sin"] = np.sin(emb).T[p % HD]
    t["dist"] = np.clip(np.arange(L)[None] - (p % L)[:, None], 0, None)
    return np.concatenate([np.asarray(t[n], np.float32).reshape(P, w) for n, w in C_ITEMS], 1)


class Shared:
    pass


class Stage:
    pass


def build(nc, A, out, stages=STAGES):
    ctx = ExitStack()
    with ctx:
        c = Shared()
        c.nc, c.A, c.out = nc, A, out
        c.sem = lambda name: ctx.enter_context(nc.semaphore(name))
        sb = lambda name, shape, dt=F32: ctx.enter_context(nc.sbuf_tensor(name, shape, dt))
        c.ps = ctx.enter_context(nc.psum_tensor("banks", [P, 8, 512], F32))
        c.w = sb("weights", [P, W_N])
        c.r = sb("rows", [P, R_N])
        c.c = sb("consts", [P, C_N])
        c.x = sb("x", [P, PAIRS, D])
        c.y = sb("y", [P, PAIRS, D])
        c.xT = sb("xT", [P, PAIRS + 1, D])
        c.o = sb("o", [P, PAIRS, D])
        c.fold = sb("fold", [P, H, D])
        c.foldv = sb("foldv", [P, H, D])
        c.kb = sb("kb", [P, H])
        c.one = sb("one", [P, 1])
        c.dec = sb("minus_5_ln2", [P, 1])
        c.spare = sb("spare", [P, 64])
        c.spared = 0
        c.eps = sb("eps", [P, 1])
        c.ARENA = 30400
        c.arena = sb("arena", [P, c.ARENA])

        def W(name, a=0, b=None):
            s, n = W_AT[name]
            return c.w[:, s + a:s + (n if b is None else b)]

        def R(name):
            s, n = R_AT[name]
            return c.r[:, s:s + n]

        def C(name):
            s, n = C_AT[name]
            return c.c[:, s:s + n]

        c.W, c.R, c.C = W, R, C
        c.loaded = ctx.enter_context(nc.semaphore("inputs_loaded"))
        c.stored = ctx.enter_context(nc.semaphore("output_stored"))
        segments = [[setup, self_attention, cross_attention_0, feed_forward, linear_attention],
                    [mixture_0, queries_1], [cross_attention_1, residual_1], [rotary_attention, mixture_1]]
        left = stages + 1
        for n, segment in enumerate(segments):
            segment = segment[:left]
            left -= len(segment)
            sems = []

            def new_sem(name):
                sems.append(nc.alloc_semaphore(name=name))
                return sems[-1]

            c.sem = new_sem
            run_segment(c, [part(c) for part in segment], last=left == 0 or n == len(segments) - 1)
            nc.clear_and_free_semaphores(sems)
            nc.all_engine_barrier()
            if left == 0:
                break


def run_segment(c, parts, last):
    nc = c.nc
    before = []
    for m in parts:
        m.before, before = before, m.after
    with nc.Block() as block:

        def run(kind, eng):
            for m in parts:
                fn = m.engines.get(kind)
                if fn is None:
                    continue
                for s, v in m.before:
                    eng.wait_ge(s, v)
                fn(eng)

        @block.sync
        def _(sp):
            run("sp", sp)
            if last:
                for s, v in before:
                    sp.wait_ge(s, v)
                sp.dma_start(c.out.rearrange("(i b) l d -> (b l) i d", b=2), c.x[:]).then_inc(c.stored, 16)
                sp.wait_ge(c.stored, 16)

        @block.tensor
        def _(pe):
            run("pe", pe)

        @block.vector
        def _(dve):
            run("dve", dve)

        @block.scalar
        def _(act):
            run("act", act)

        @block.gpsimd
        def _(pool):
            run("pool", pool)


class Carver:

    def __init__(self, c):
        self.c, self.at = c, 0

    def f32(self, *shape):
        n = int(np.prod(shape))
        v = self.c.arena[:, self.at:self.at + n]
        self.at += n
        assert self.at <= self.c.ARENA, self.at
        if len(shape) > 1:
            names = "abcd"[:len(shape)]
            v = v.rearrange(f"p ({' '.join(names)}) -> p {' '.join(names)}", **dict(zip(names[1:], shape[1:])))
        return v

    def bf16(self, *shape):
        n = -(-int(np.prod(shape)) // 2)
        v = self.c.arena[:, self.at:self.at + n].bitcast(BF16)
        self.at += n
        assert self.at <= self.c.ARENA, self.at
        if len(shape) > 1:
            names = "abcd"[:len(shape)]
            v = v.rearrange(f"p ({' '.join(names)}) -> p {' '.join(names)}", **dict(zip(names[1:], shape[1:])))
        return v


def nth(g, j, per=G):
    return g * per + (j + 1)


def spread(ap, n, axis=2):
    if axis == 2:
        return ap.unsqueeze(2).to_broadcast([P, ap.shape[1], n])
    return ap.unsqueeze(1).to_broadcast([P, n, ap.shape[1]])


def setup(c):
    A = c.A
    m = Stage()
    folded = c.sem("weights_folded_psum")
    foldc = c.sem("weights_folded")
    masked = c.sem("masked_wq_ready")
    k = Carver(c)
    wqm = k.f32(2, D)
    bqm = k.f32(H)
    bqm_ready = c.sem("masked_bq_ready")
    zero = c.sem("xT_pad_zero")

    def sp(eng):
        eng.dma_start(c.w[:], A["weights"]).then_inc(c.loaded, 16)
        eng.dma_start(c.r[:], A["rows"]).then_inc(c.loaded, 16)
        eng.dma_start(c.c[:], A["consts"]).then_inc(c.loaded, 16)
        eng.dma_start(c.x[:], A["x"].rearrange("(i b) l d -> (b l) i d", b=2)).then_inc(c.loaded, 16)

    def pool(eng):
        eng.memset(c.xT[:, PAIRS, :], 0.0).then_inc(zero, 1)
        eng.memset(c.one[:], 1.0).then_inc(zero, 1)
        eng.memset(c.dec[:], -5.0 * LN2).then_inc(zero, 1)
        eng.memset(c.eps[:], EPS).then_inc(zero, 1)

    def dve(eng):
        eng.wait_ge(c.loaded, 64)
        eng.tensor_scalar(bqm, c.C("head8"), c.W("c_bq"), None, ALU.mult).then_inc(bqm_ready, 1)
        for h in range(H):
            if h >= 2:
                eng.wait_ge(folded, h - 1)
            eng.tensor_scalar(wqm[:, h % 2, :], c.W("c_wq"), c.C("head8")[:, h:h + 1], None,
                              ALU.mult).then_inc(masked, 1)

    def pe(eng):
        eng.wait_ge(c.loaded, 64)
        for h in range(H):
            eng.wait_ge(masked, h + 1)
            eng.matmul(c.ps[:, h // 4, (h % 4) * D:(h % 4 + 1) * D], wqm[:, h % 2, :], c.W("c_wk"),
                       start=True, stop=True).then_inc(folded, 1)
        eng.wait_ge(bqm_ready, 1)
        eng.matmul(c.ps[:, 4, 0:H], c.W("c_wk"), bqm, start=True, stop=True).then_inc(folded, 1)

    def act(eng):
        eng.wait_ge(folded, H + 1)
        for q in range(4):
            eng.activation(c.fold[:, 4 * q:4 * q + 4, :], c.ps[:, q, :].rearrange("p (h d) -> p h d", d=D),
                           ACT.Copy).then_inc(foldc, 1)
        eng.activation(c.kb[:], c.ps[:, 4, 0:H], ACT.Copy).then_inc(foldc, 1)

    m.engines = dict(sp=sp, pool=pool, dve=dve, pe=pe, act=act)
    m.after = [(foldc, 5), (c.loaded, 64), (zero, 4)]
    return m


def settle(c, dve):
    n = c.spared % 64
    dve.memset(c.spare[:, n:n + 1], 0.0)
    c.spared += 1


def wait_if(eng, sem, value):
    if not isinstance(value, int) or value > 0:
        eng.wait_ge(sem, value)


class Norm:

    def __init__(self, c, k, name, affine=None):
        self.c, self.affine = c, affine
        self.stats = k.f32(G, 6)
        self.mv = k.f32(G, 2)
        self.rstd = k.f32(G, 1)
        self.s_stats, self.s_mv, self.s_rstd = (c.sem(f"{name}_{n}") for n in ("stats", "mean_var", "rstd"))
        self.log = k.f32(G)
        self.s_log = c.sem(f"{name}_log")
        self.ready = c.sem(f"{name}_ready")
        if affine:
            self.s_n, self.s_g = c.sem(f"{name}_normed"), c.sem(f"{name}_scaled")

    def dve(self, eng, g, src, dst, wait=None):
        for j in range(G):
            if wait:
                wait(j)
            eng.bn_stats(self.stats[:, j, :], src(j)).then_inc(self.s_stats, 1)
        for j in range(G):
            eng.wait_ge(self.s_stats, nth(g, j))
            settle(self.c, eng)
            eng.bn_aggr(self.mv[:, j, :], self.stats[:, j, :]).then_inc(self.s_mv, 1)
        last = self.s_n if self.affine else self.ready
        for j in range(G):
            if j == 0:
                eng.wait_ge(self.s_rstd, g + 1)
            eng.tensor_scalar(dst(j), src(j), self.mv[:, j, 0:1], self.rstd[:, j, :], ALU.subtract,
                              ALU.mult).then_inc(last, 1)
        if self.affine:
            for j in range(G):
                eng.wait_ge(self.s_n, nth(g, j))
                eng.tensor_tensor(dst(j), dst(j), self.c.R(self.affine[0]), ALU.mult).then_inc(self.s_g, 1)
            for j in range(G):
                eng.wait_ge(self.s_g, nth(g, j))
                eng.tensor_tensor(dst(j), dst(j), self.c.R(self.affine[1]), ALU.add).then_inc(self.ready, 1)


    def act(self, eng, g):
        eng.wait_ge(self.s_mv, g * G + G)
        eng.activation(self.log, self.mv[:, :, 1], ACT.Ln, bias=self.c.eps[:, 0:1]).then_inc(self.s_log, 1)
        eng.wait_ge(self.s_log, g + 1)
        eng.activation(self.rstd[:, :, 0], self.log, ACT.Exp, scale=-0.5).then_inc(self.s_rstd, 1)


class Turn:

    def __init__(self, c, name):
        self.c = c
        self.ps, self.ready = c.sem(f"{name}_psum"), c.sem(f"{name}_ready")

    def pe(self, eng, g, src, bank, made):
        for j in range(G):
            eng.wait_ge(made, nth(g, j))
            eng.transpose(bank(j), src(j), self.c.C("ident")).then_inc(self.ps, 1)

    def act(self, eng, g, bank, dst, **kw):
        for j in range(G):
            eng.wait_ge(self.ps, nth(g, j))
            eng.activation(dst(j), bank(j), ACT.Identity if kw else ACT.Copy, **kw).then_inc(self.ready, 1)


class HeadMix:

    def __init__(self, c, k, name):
        self.c = c
        self.spread = k.f32(G, 2, H * L)
        self.pt = k.f32(G, 2 * 512)
        self.vals = k.f32(G, 2 * D)
        n = lambda s: c.sem(f"{name}_{s}")
        self.s_spread, self.s_vps, self.s_vals, self.s_scores = n("keys_spread"), n("values_psum"), n("values"), n("scores")
        self.s_ptps, self.s_pt, self.s_o = n("probs_turned_psum"), n("probs_turned"), n("heads_psum")

    def pool_spread(self, eng, g, keysT, made):
        c = self.c
        for j in range(G):
            eng.wait_ge(made, nth(g, j))
            for b in range(2):
                eng.tensor_tensor(self.spread[:, j, b, :].rearrange("p (h q) -> p h q", h=H),
                                  spread(keysT(j)[:, b * L:(b + 1) * L], H, 1), spread(c.C("head8"), L),
                                  ALU.mult).then_inc(self.s_spread, 1)

    def pe_values(self, eng, g, xT, made, weight):
        c = self.c
        for j in range(G):
            eng.wait_ge(made, nth(g, j))
            for b in range(2):
                for h2 in range(2):
                    mm = eng.matmul(c.ps[h2 * L:(h2 + 1) * L, 2 * j + 1, b * D:(b + 1) * D],
                                    xT(j)[:, b * L:(b + 1) * L], weight, start=True, stop=True)
            mm.then_inc(self.s_vps, 1)

    def dve_values(self, eng, g):
        c = self.c
        for j in range(G):
            eng.wait_ge(self.s_vps, nth(g, j))
            half = c.C("half").unsqueeze(1).unsqueeze(3).to_broadcast([P, 2 * HP, 2, HD])
            v = lambda a: a.rearrange("p (x h d) -> p x h d", h=2, d=HD)
            eng.tensor_tensor(v(self.vals[:, j, :]), v(c.ps[:, 2 * j + 1, 0:2 * D]), half,
                              ALU.mult).then_inc(self.s_vals, 1)

    def pe_scores(self, eng, g, qT, made, bank_free):
        c = self.c
        for j in range(G):
            eng.wait_ge(made, nth(g, j))
            eng.wait_ge(self.s_vals, nth(g, j))
            eng.wait_ge(self.s_spread, nth(g, 2 * j + 1, 2 * G))
            for b in range(2):
                for x in range(2):
                    mm = eng.matmul(c.ps[b * L:(b + 1) * L, 2 * j + x, :], qT(j)[:, b * L:(b + 1) * L],
                                    self.spread[:, j, b, x * 512:(x + 1) * 512], start=True, stop=True)
            mm.then_inc(self.s_scores, 1)

    def pe_turn(self, eng, g, probs, made, scores_read):
        c = self.c
        for j in range(G):
            eng.wait_ge(scores_read, nth(g, j))
            eng.wait_ge(made, nth(g, j))
            for hp in range(HP):
                mm = eng.transpose(c.ps[:, 2 * j + hp // 4, (hp % 4) * P:(hp % 4 + 1) * P],
                                   probs(j)[:, hp * P:(hp + 1) * P], c.C("ident"))
            mm.then_inc(self.s_ptps, 1)

    def act_turn(self, eng, g):
        c = self.c
        for j in range(G):
            eng.wait_ge(self.s_ptps, nth(g, j))
            eng.activation(self.pt[:, j, :].rearrange("p (x n) -> p x n", x=2), c.ps[:, 2 * j:2 * j + 2, :],
                           ACT.Copy).then_inc(self.s_pt, 1)

    def pe_mix(self, eng, g):
        c = self.c
        for j in range(G):
            eng.wait_ge(self.s_pt, nth(g, j))
            for b in range(2):
                for hp in range(HP):
                    mm = eng.matmul(c.ps[b * L:(b + 1) * L, 2 * j, hp * 2 * HD:(hp + 1) * 2 * HD],
                                    self.pt[:, j, hp * P + b * L:hp * P + (b + 1) * L],
                                    self.vals[:, j, b * D + hp * 2 * HD:b * D + (hp + 1) * 2 * HD],
                                    start=True, stop=True)
            mm.then_inc(self.s_o, 1)


def heads(ap, h=H):
    return ap.rearrange("p (h d) -> p h d", h=h)


def self_attention(c):
    m = Stage()
    k = Carver(c)
    xn, xT = k.f32(G, D), k.f32(G, D)
    sc = k.f32(G, H, L + PAD)
    rest = k.f32(G, H, L + PAD)
    m8 = k.f32(G, H, 8)
    pr = k.f32(G, H * L)
    den, rden = k.f32(G, H), k.f32(G, H)
    on, oT, t = k.f32(G, D), k.f32(G, D), k.f32(G, D)
    pre, ln1 = Norm(c, k, "sa_pre"), Norm(c, k, "sa_ln1", ("ln1_g", "ln1_b"))
    turn, turno, turny = Turn(c, "sa_xT"), Turn(c, "sa_oT"), Turn(c, "sa_yT")
    mix = HeadMix(c, k, "sa")
    s = {n: c.sem(f"sa_{n}") for n in ("sentinels", "scores_copied", "top8", "marked", "shifted", "exps", "probs",
                                       "sums", "recips", "heads", "proj", "added", "biased", "y_kept")}
    A_ = lambda j: c.ps[:, 2 * j, 0:P]
    B_ = lambda j: c.ps[:, 2 * j + 1, 0:P]

    def dve(eng):
        eng.memset(sc[:].rearrange("p g h n -> p (g h) n")[:, :, L:L + PAD], BIG).then_inc(s["sentinels"], 1)
        with eng.Fori(0, GROUPS) as g:
            eng.wait_ge(turny.ready, g * G)
            eng.wait_ge(s["y_kept"], g * G)
            pre.dve(eng, g, lambda j: c.x[:, g * G + j, :], rows(xn))
            mix.dve_values(eng, g)
            for j in range(G):
                eng.wait_ge(s["sentinels"], 1)
                eng.wait_ge(s["scores_copied"], nth(g, j))
                for h in range(H):
                    i = eng.max(m8[:, j, h, :], sc[:, j, h, :])
                i.then_inc(s["top8"], 1)
            for j in range(G):
                eng.wait_ge(s["top8"], nth(g, j))
                settle(c, eng)
                for h in range(H):
                    i = eng.match_replace(rest[:, j, h, :], m8[:, j, h, :], sc[:, j, h, :], GONE)
                i.then_inc(s["marked"], 1)
            for j in range(G):
                eng.wait_ge(s["marked"], nth(g, j))
                eng.wait_ge(s["exps"], nth(g, j))
                eng.scalar_tensor_tensor(out=heads(pr[:, j, :]), in0=rest[:, j, :, 0:L], scalar=GONE / 2,
                                         in1=heads(pr[:, j, :]), op0=ALU.is_le, op1=ALU.mult).then_inc(s["probs"], 1)
            for j in range(G):
                eng.wait_ge(s["probs"], nth(g, j))
                eng.tensor_reduce(den[:, j, :], heads(pr[:, j, :]), AX, ALU.add).then_inc(s["sums"], 1)
            for j in range(G):
                eng.wait_ge(s["sums"], nth(g, j))
                eng.reciprocal(rden[:, j, :], den[:, j, :]).then_inc(s["recips"], 1)
            for j in range(G):
                eng.wait_ge(s["recips"], nth(g, j))
                eng.wait_ge(mix.s_o, nth(g, j))
                eng.tensor_tensor(heads(on[:, j, :]), heads(A_(j)), spread(rden[:, j, :], HD),
                                  ALU.mult).then_inc(s["heads"], 1)
            for j in range(G):
                eng.wait_ge(s["proj"], nth(g, j))
                eng.tensor_tensor(t[:, j, :], A_(j), xn[:, j, :], ALU.add).then_inc(s["added"], 1)
            for j in range(G):
                eng.wait_ge(s["added"], nth(g, j))
                eng.tensor_tensor(t[:, j, :], t[:, j, :], c.R("self_out_b"), ALU.add).then_inc(s["biased"], 1)
            ln1.dve(eng, g, rows(t), rows(on), wait=lambda j: (eng.wait_ge(s["biased"], nth(g, j)),
                                                              eng.wait_ge(turno.ready, nth(g, j))))

    def pe(eng):
        with eng.Fori(0, GROUPS) as g:
            eng.wait_ge(turny.ready, g * G)
            turn.pe(eng, g, rows(xn), A_, pre.ready)
            mix.pe_values(eng, g, rows(xT), turn.ready, c.C("ident"))
            mix.pe_scores(eng, g, rows(xT), turn.ready, None)
            mix.pe_turn(eng, g, rows(pr), s["probs"], s["scores_copied"])
            mix.pe_mix(eng, g)
            turno.pe(eng, g, rows(on), B_, s["heads"])
            for j in range(G):
                eng.wait_ge(turno.ready, nth(g, j))
                eng.matmul(A_(j), oT[:, j, :], c.W("self_out"), start=True, stop=True).then_inc(s["proj"], 1)
            turny.pe(eng, g, rows(on), B_, ln1.ready)

    def act(eng):
        with eng.Fori(0, GROUPS) as g:
            eng.wait_ge(s["y_kept"], g * G)
            pre.act(eng, g)
            turn.act(eng, g, A_, rows(xT))
            for j in range(G):
                eng.wait_ge(s["sentinels"], 1)
                eng.wait_ge(mix.s_scores, nth(g, j))
                eng.activation(sc[:, j, :, 0:L], c.ps[:, 2 * j:2 * j + 2, :].rearrange("p x (h n) -> p (x h) n", n=L),
                               ACT.Copy).then_inc(s["scores_copied"], 1)
            for j in range(G):
                eng.wait_ge(s["shifted"], nth(g, j))
                eng.activation(pr[:, j, :], pr[:, j, :], ACT.Exp, scale=D ** -0.5).then_inc(s["exps"], 1)
            mix.act_turn(eng, g)
            turno.act(eng, g, B_, rows(oT))
            ln1.act(eng, g)
            turny.act(eng, g, B_, lambda j: c.xT[:, g * G + j, :])

    def pool(eng):
        with eng.Fori(0, GROUPS) as g:
            mix.pool_spread(eng, g, rows(xT), turn.ready)
            for j in range(G):
                eng.wait_ge(s["top8"], nth(g, j))
                eng.tensor_tensor(heads(pr[:, j, :]), sc[:, j, :, 0:L],
                                  m8[:, j, :, PAD:PAD + 1].to_broadcast([P, H, L]),
                                  ALU.subtract).then_inc(s["shifted"], 1)
            for j in range(G):
                eng.wait_ge(ln1.ready, nth(g, j))
                eng.tensor_copy(c.y[:, g * G + j, :], on[:, j, :]).then_inc(s["y_kept"], 1)

    m.engines = dict(pe=pe, dve=dve, act=act, pool=pool)
    m.after = [(turny.ready, PAIRS), (s["y_kept"], PAIRS)]
    return m



def cross_attention(c, layer):
    m = Stage()
    nm = f"x{layer}"
    scale = (HD if layer == 0 else XD) ** -0.5
    k = Carver(c)
    ctxT = k.f32(2, S)
    ch, cl = k.bf16(2, S + 1), k.bf16(2, S + 1)
    qf = k.f32(2, H * L)
    qh, ql = k.bf16(2, H * L), k.bf16(2, H * L)
    sm = k.f32(4, S)
    pt = k.f32(2, KT * P)
    mx, nmx = k.f32(4, 2), k.f32(4, 1)
    den, rden = k.f32(2, HP), k.f32(2, HP)
    if layer == 0:
        vals = k.f32(2, KT * D)
        om = k.f32(D)
        on = k.f32(D)
    else:
        ctxn = k.f32(2, KT * D)
        mrow = k.bf16(2, S + 1)
        mrow8 = mrow.bitcast(U8)
        hide = k.f32(2, S)
        u = k.f32(2, D)
        acc = k.f32(2, D)
    sem = lambda n: c.sem(f"{nm}_{n}")
    two = lambda n: [sem(f"{n}{i}") for i in range(2)]
    loaded = two("ctxT_loaded")
    split = two("ctx_split")
    low_ready, q_high = sem("ctx_high"), sem("queries_high")
    qsplit = two("queries_split")
    qf_made = two("queries_made")
    scored = [sem("scores_a"), sem("scores_b")]
    taken = [sem("scores_taken_a"), sem("scores_taken_b")]
    shift = sem("shift_ready")
    exps = sem("probs_ready")
    turned = [sem(f"probs_turned{i}") for i in range(4)]
    tp = [sem(f"turned_psum{i}") for i in range(3)]
    tg = [sem(f"turned_group{i}") for i in range(4)]
    mixed = two("mixed_tile")
    small = sem("small_psum")
    recips = sem("recips")
    if layer == 0:
        omasked, oscaled, vals_made = sem("mix_masked"), sem("mix_scaled"), two("values_made")
    else:
        nloaded, mloaded, hidden = two("ctx_loaded"), two("mask_loaded"), two("mask_ready")
        umade, accd = sem("mix_copied"), sem("sum_made")
    out_made = sem("out_made")
    chunks = [(0, 512), (512, 1024), (1024, 1536), (1536, S)]
    halves = [(0, 1024), (1024, S)]
    T = 2 * HP

    def small_tasks(slot, more):
        r = []
        if layer == 0:
            if slot == HP:
                r.append(("o", 0))
            if slot % HP in (1, 3, 5, 6):
                r.append(("v", slot // HP ^ 1, {1: 0, 3: 1, 5: 2, 6: 3}[slot % HP]))
        elif slot >= 1:
            r.append(("y", slot - 1))
            if slot == HP:
                r.append(("f", 0))
        if slot % HP in (2, 4):
            r.append(("q", slot // HP ^ 1, slot % HP // 2 - 1))
        return [x for x in r if more or slot < HP or x[0] not in "vq"]

    def last_tasks():
        return [("o", 1)] if layer == 0 else [("y", T - 1), ("f", 1)]

    first = [("q", 0, 0), ("q", 0, 1)] + ([("v", 0, x) for x in range(4)] if layer == 0 else [])
    per = sum(len(small_tasks(s, True)) for s in range(T)) + len(last_tasks())

    def order(i, more, do_slot, do_task):
        n = len(first) + i * per
        for s in range(T):
            tasks = small_tasks(s, more)
            do_slot(s, [(n + x, t) for x, t in enumerate(tasks)])
            n = n + len(tasks)
        for x, t in enumerate(last_tasks()):
            do_task(n + x, t, T)

    def pairs(eng, body):
        with eng.Fori(0, PAIRS - 1) as i:
            body(i, True)
        body(PAIRS - 1, False)

    def wait_scored(eng, i, b):
        wait_if(eng, scored[1], (i - 1) * T + (b + 1) * HP)

    def wait_mixed(eng, i, b):
        wait_if(eng, mixed[1], i * HP + (b + 1) * (HP // 2))

    def taken_small(i, tk, slot):
        kind = tk[0]
        if kind == "q":
            return qf_made[tk[1]], nxt(i, tk[1], slot) * 2 + tk[2] + 1
        if kind == "v":
            return vals_made[tk[1]], nxt(i, tk[1], slot) * 4 + tk[2] + 1
        if kind == "y":
            return accd, i * T + tk[1] + 1
        return out_made, i * 2 + tk[1] + 1

    def nxt(i, b, slot):
        return i if slot < HP else i + 1

    def sp(eng):
        n = (KT - 1) * P

        def load(i, b):
            held = (lambda v: v if isinstance(i, int) else eng.snap(v))
            last, made, bb, i = (held((i - 1) * HP + (b + 1) * (HP // 2)), held(i * 4), held(i * 2 + b), held(i * 1))
            if layer == 0:
                wait_if(eng, vals_made[b], made)
            else:
                wait_if(eng, hidden[b], i)
            wait_if(eng, split[b], i)
            eng.wait_ge(c.loaded, 64)
            eng.dma_start(ctxT[:, b, :], c.A["ctxT"][bass.ds(bb, 1), :, :].rearrange("o d s -> (o d) s"))\
               .then_inc(loaded[b], 16)
            if layer == 1:
                eng.dma_start(mrow8[:, b, 0:S], c.A["mask"][bass.ds(bb, 1), :].to_broadcast([P, S]))\
                   .then_inc(mloaded[b], 16)
                wait_if(eng, mixed[1], last)
                eng.wait_ge(c.loaded, 64)
                eng.dma_start(ctxn[:, b, 0:n].rearrange("p (t d) -> p t d", d=D),
                              c.A["ctx"][bass.ds(bb, 1), 0:n, :].rearrange("o (t p) d -> (o p) t d", p=P))\
                   .then_inc(nloaded[b], 16)
                eng.dma_start(ctxn[0:KL, b, n:n + D],
                              c.A["ctx"][bass.ds(bb, 1), n:S, :].rearrange("o p d -> (o p) d"))\
                   .then_inc(nloaded[b], 16)

        load(0, 0)

        def body(i, more):
            load(i, 1)
            if more:
                load(i + 1, 0)
        pairs(eng, body)

    def pool(eng):
        def split_queries(i, b):
            wait_scored(eng, i, b)
            eng.wait_ge(qf_made[b], i * 2 + 2)
            eng.tensor_tensor(qh[:, b, :], qf[:, b, :], c.one[:].to_broadcast([P, H * L]), ALU.mult).then_inc(q_high, 1)
            eng.wait_ge(q_high, i * 2 + b + 1)
            eng.tensor_tensor(ql[:, b, :], qf[:, b, :], qh[:, b, :], ALU.subtract).then_inc(qsplit[b], 1)

        def split_context(i, b):
            eng.wait_ge(loaded[b], i * 16 + 16)
            wait_scored(eng, i, b)
            if layer == 1:
                wait_if(eng, taken[1], (i - 1) * T + (b + 1) * HP)
                eng.wait_ge(mloaded[b], i * 16 + 16)
            eng.tensor_tensor(ch[:, b, 0:S], ctxT[:, b, :], c.one[:].to_broadcast([P, S]), ALU.mult).then_inc(low_ready, 1)
            eng.wait_ge(low_ready, i * 2 + b + 1)
            eng.tensor_tensor(cl[:, b, 0:S], ctxT[:, b, :], ch[:, b, 0:S], ALU.subtract).then_inc(split[b], 1)
            if layer == 1:
                eng.tensor_scalar(hide[:, b, :], mrow8[:, b, 0:S], -1.0, -GONE, ALU.add, ALU.mult).then_inc(hidden[b], 1)

        split_context(0, 0)
        split_queries(0, 0)

        def body(i, more):
            split_context(i, 1)
            split_queries(i, 1)
            if more:
                split_context(i + 1, 0)
                split_queries(i + 1, 0)
        pairs(eng, body)

    def pe(eng):
        def scores(i, t, half):
            b, hp = t // HP, t % HP
            if t % HP == 0 and half == 0:
                eng.wait_ge(split[b], i + 1)
                eng.wait_ge(qsplit[b], i + 1)
            eng.wait_ge(taken[half], i * T + t)
            q = slice(hp * P, (hp + 1) * P)
            for n in (2 * half, 2 * half + 1):
                a, z = chunks[n]
                o = c.ps[:, n, 0:z - a]
                eng.matmul(o, qh[:, b, q], ch[:, b, a:z], start=True, stop=False)
                eng.matmul(o, qh[:, b, q], cl[:, b, a:z], start=False, stop=False)
                mm = eng.matmul(o, ql[:, b, q], ch[:, b, a:z], start=False, stop=True)
            mm.then_inc(scored[half], 1)

        def turn(i, t, gr):
            if gr == 0:
                eng.wait_ge(exps, i * T + t + 1)
            eng.wait_ge(tg[(gr + 2) % 4], i * T + t + gr // 2)
            kts = range(4 * gr, min(4 * gr + 4, KT))
            for kt in kts:
                w = P if kt < KT - 1 else KL
                mm = eng.transpose(c.ps[0:w, 4 + gr % 2, (kt % 4) * P:(kt % 4 + 1) * P],
                                   sm[:, t % 4, kt * P:kt * P + w], c.C("ident"))
            mm.then_inc(tp[gr] if gr < 3 else turned[t % 4], 1)

        def mix(i, t, gr):
            b, hp = t // HP, t % HP
            eng.wait_ge(tg[gr], i * T + t + 1)
            if gr == 0:
                if layer == 0:
                    if hp == 0:
                        eng.wait_ge(vals_made[b], i * 4 + 4)
                        eng.wait_ge(omasked, i * 2 + b)
                else:
                    if hp == 0:
                        eng.wait_ge(nloaded[b], i * 32 + 32)
                    eng.wait_ge(umade, i * T + t)
            for kt in range(4 * gr, min(4 * gr + 4, KT)):
                w = P if kt < KT - 1 else KL
                kw = dict(start=kt == 0, stop=kt == KT - 1)
                ptk = pt[0:w, t % 2, kt * P:(kt + 1) * P]
                if layer == 0:
                    mm = eng.matmul(c.ps[:, 7, hp * 2 * HD:(hp + 1) * 2 * HD], ptk,
                                    vals[0:w, b, kt * D + hp * 2 * HD:kt * D + (hp + 1) * 2 * HD], **kw)
                else:
                    mm = eng.matmul(c.ps[:, 7, 0:P], ctxn[0:w, b, kt * D:(kt + 1) * D], ptk, **kw)
            if gr == 3:
                mm.then_inc(mixed[t % 2], 1)

        def task(i, n, tk, slot):
            kind = tk[0]
            if last["use"] is not None:
                eng.wait_ge(*taken_small(*last["use"]))
            last["use"] = (i, tk, slot)
            if kind == "q":
                _, b, x = tk
                p = nxt(i, b, slot)
                for h in range(8):
                    mm = eng.matmul(c.ps[:, 6, h * L:(h + 1) * L], c.fold[:, 8 * x + h, :],
                                    c.xT[:, p, b * L:(b + 1) * L], start=True, stop=True)
            elif kind == "v":
                _, b, x = tk
                if x == 0:
                    eng.wait_ge(loaded[b], nxt(i, b, slot) * 16 + 16)
                for kt in range(4 * x, min(4 * x + 4, KT)):
                    w = P if kt < KT - 1 else KL
                    mm = eng.matmul(c.ps[0:w, 6, (kt % 4) * P:(kt % 4 + 1) * P], ctxT[:, b, kt * P:kt * P + w],
                                    c.W("c_wv"), start=True, stop=True)
            elif kind == "o":
                eng.wait_ge(oscaled, i * 2 + tk[1] + 1)
                mm = eng.matmul(c.ps[:, 6, 0:L], on, c.C("stack"), start=True, stop=True)
            elif kind == "y":
                t = tk[1]
                eng.wait_ge(umade, i * T + t + 1)
                for h2 in range(2):
                    mm = eng.matmul(c.ps[h2 * L:(h2 + 1) * L, 6, 0:D], u[:, t % 2, h2 * L:(h2 + 1) * L],
                                    c.foldv[:, 2 * (t % HP) + h2, :], start=True, stop=True)
            else:
                b = tk[1]
                mm = eng.matmul(c.ps[b * L:(b + 1) * L, 6, 0:D], c.C("stack"), acc[:, b, :], start=True, stop=True)
            mm.then_inc(small, 1)

        last = dict(use=None)
        for n, tk in enumerate(first):
            task(0, n, tk, 0)
        eng.wait_ge(*taken_small(*last["use"]))
        scores(0, 0, 0)
        scores(0, 0, 1)

        def body(i, more):
            last["use"] = (i - 1, last_tasks()[-1], T)
            def slot(t, tasks):
                ahead = (i, t + 1) if t + 1 < T else ((i + 1, 0) if more else None)
                if ahead:
                    scores(*ahead, 0)
                turn(i, t, 0)
                turn(i, t, 1)
                if ahead:
                    scores(*ahead, 1)
                turn(i, t, 2)
                turn(i, t, 3)
                for n, tk in tasks:
                    task(i, n, tk, t)
                for gr in range(4):
                    mix(i, t, gr)
            order(i, more, slot, lambda n, tk, s: task(i, n, tk, s))
        pairs(eng, body)

    def take(eng, copy, i, t, gr):
        if gr < 3:
            eng.wait_ge(tp[gr], i * T + t + 1)
        else:
            eng.wait_ge(turned[t % 4], i * 4 + t // 4 + 1)
        eng.wait_ge(mixed[t % 2], i * HP + t // 2)
        if gr < 3:
            o, s = pt[:, t % 2, gr * 512:(gr + 1) * 512], c.ps[:, 4 + gr % 2, :]
        else:
            o, s = pt[0:KL, t % 2, 1536:1536 + P], c.ps[0:KL, 5, 0:P]
        copy(o, s).then_inc(tg[gr], 1)

    def dve(eng):
        def maxima(i, t, half):
            a, z = halves[half]
            eng.wait_ge(scored[half], i * T + t + 1)
            if half == 0:
                eng.wait_ge(turned[t % 4], i * 4 + t // 4)
                if layer == 1 and t % HP == 0:
                    eng.wait_ge(hidden[t // HP], i + 1)
            src = c.ps[:, 2 * half:2 * half + 2, :].rearrange("p x n -> p (x n)")[:, 0:z - a]
            if layer == 0:
                eng.tensor_scalar(sm[:, t % 4, a:z], src, 1.0, -BIG, ALU.mult, ALU.max,
                                  accum_out=mx[:, t % 4, half:half + 1]).then_inc(taken[half], 1)
            else:
                settle(c, eng)
                eng.tensor_tensor_reduce(out=sm[:, t % 4, a:z], in0=src, in1=hide[:, t // HP, a:z], scale=1.0,
                                         scalar=-BIG, op0=ALU.add, op1=ALU.max,
                                         accum_out=mx[:, t % 4, half:half + 1]).then_inc(taken[half], 1)
            if half == 1:
                eng.wait_ge(taken[0], i * T + t + 1)
                eng.wait_ge(taken[1], i * T + t + 1)
                eng.tensor_scalar(nmx[:, t % 4, :], mx[:, t % 4, 0:1], mx[:, t % 4, 1:2], -scale, ALU.max,
                                  ALU.mult).then_inc(shift, 1)

        def task(i, n, tk, slot):
            kind = tk[0]
            if kind == "q":
                _, b, x = tk
                p = nxt(i, b, slot)
                eng.wait_ge(small, n + 1)
                eng.wait_ge(qsplit[b], p)
                o = qf[:, b, x * 512:(x + 1) * 512].rearrange("p (h q) -> p h q", q=L)
                s = c.ps[:, 6, :].rearrange("p (h q) -> p h q", q=L)
                if layer == 0:
                    ins = eng.tensor_tensor(o, s, spread(c.kb[:, 8 * x:8 * x + 8], L), ALU.add)
                else:
                    ins = eng.tensor_copy(o, s)
                ins.then_inc(qf_made[b], 1)
            elif kind == "y":
                t = tk[1]
                b, hp = t // HP, t % HP
                eng.wait_ge(exps, i * T + t + 1)
                eng.reciprocal(rden[:, b, hp:hp + 1], den[:, b, hp:hp + 1]).then_inc(recips, 1)
                eng.wait_ge(recips, i * T + t + 1)
                eng.wait_ge(small, n + 1)
                if hp == 0:
                    eng.wait_ge(out_made, i * 2 + b)
                    ins = eng.tensor_scalar(acc[:, b, :], c.ps[:, 6, 0:D], rden[:, b, hp:hp + 1], None, ALU.mult)
                else:
                    eng.wait_ge(accd, i * T + t)
                    ins = eng.scalar_tensor_tensor(out=acc[:, b, :], in0=c.ps[:, 6, 0:D], scalar=rden[:, b, hp:hp + 1],
                                                   in1=acc[:, b, :], op0=ALU.mult, op1=ALU.add)
                ins.then_inc(accd, 1)

        def mix_out(i, b):
            wait_mixed(eng, i, b)
            v = lambda a: a.rearrange("p (x h d) -> p x h d", h=2, d=HD)
            eng.wait_ge(out_made, i * 2 + b)
            eng.tensor_tensor(v(om), v(c.ps[:, 7, 0:D]),
                              c.C("half").unsqueeze(1).unsqueeze(3).to_broadcast([P, HP, 2, HD]),
                              ALU.mult).then_inc(omasked, 1)
            eng.reciprocal(rden[:, b, :], den[:, b, :]).then_inc(recips, 1)
            eng.wait_ge(omasked, i * 2 + b + 1)
            eng.wait_ge(recips, i * 2 + b + 1)
            eng.tensor_tensor(heads(on, HP), heads(om, HP), spread(rden[:, b, :], 2 * HD), ALU.mult).then_inc(oscaled, 1)

        for n, tk in enumerate(first):
            task(0, n, tk, 0)
        maxima(0, 0, 0)
        maxima(0, 0, 1)

        def body(i, more):
            def slot(t, tasks):
                if layer == 0 and t == HP:
                    mix_out(i, 0)
                ahead = (i, t + 1) if t + 1 < T else ((i + 1, 0) if more else None)
                if ahead:
                    maxima(*ahead, 0)
                    maxima(*ahead, 1)
                take(eng, lambda o, s: eng.tensor_copy(o, s), i, t, 2)
                take(eng, lambda o, s: eng.tensor_copy(o, s), i, t, 3)
                for n, tk in tasks:
                    task(i, n, tk, t)
            def tail(n, tk, s):
                if layer == 0:
                    mix_out(i, 1)
                task(i, n, tk, s)
            order(i, more, slot, tail)
        pairs(eng, body)

    def act(eng):
        def exp(i, t):
            eng.wait_ge(shift, i * T + t + 1)
            if layer == 0 and t % HP == 0:
                eng.wait_ge(recips, i * 2 + t // HP)
            eng.activation(sm[:, t % 4, :], sm[:, t % 4, :], ACT.Exp, bias=nmx[:, t % 4, :], scale=scale,
                           accum_out=den[:, t // HP, t % HP:t % HP + 1]).then_inc(exps, 1)

        def task(i, n, tk, slot):
            kind = tk[0]
            if kind == "v":
                _, b, x = tk
                eng.wait_ge(small, n + 1)
                wait_mixed(eng, nxt(i, b, slot) - 1, b)
                if x < 3:
                    o, s = vals[:, b, x * 512:(x + 1) * 512], c.ps[:, 6, :]
                else:
                    o, s = vals[0:KL, b, 1536:1536 + P], c.ps[0:KL, 6, 0:P]
                eng.activation(o, s, ACT.Copy).then_inc(vals_made[b], 1)
            elif kind == "o":
                eng.wait_ge(small, n + 1)
                b = tk[1]
                eng.activation(c.o[:, i, b * L:(b + 1) * L], c.ps[:, 6, 0:L], ACT.Identity,
                               bias=c.W("c_bv")).then_inc(out_made, 1)
            elif kind == "f":
                eng.wait_ge(small, n + 1)
                b = tk[1]
                eng.activation(c.o[b * L:(b + 1) * L, i, :], c.ps[b * L:(b + 1) * L, 6, 0:D],
                               ACT.Copy).then_inc(out_made, 1)

        def copy_mix(i, t):
            eng.wait_ge(mixed[t % 2], i * HP + t // 2 + 1)
            eng.wait_ge(accd, i * T + t - 1 if t >= 1 else i * T)
            eng.activation(u[:, t % 2, :], c.ps[:, 7, 0:P], ACT.Copy).then_inc(umade, 1)

        for n, tk in enumerate(first):
            task(0, n, tk, 0)
        exp(0, 0)

        def body(i, more):
            def slot(t, tasks):
                take(eng, lambda o, s: eng.activation(o, s, ACT.Copy), i, t, 0)
                take(eng, lambda o, s: eng.activation(o, s, ACT.Copy), i, t, 1)
                ahead = (i, t + 1) if t + 1 < T else ((i + 1, 0) if more else None)
                if layer == 0:
                    if ahead:
                        exp(*ahead)
                    for n, tk in tasks:
                        task(i, n, tk, t)
                else:
                    for n, tk in tasks:
                        task(i, n, tk, t)
                    if ahead:
                        exp(*ahead)
                    copy_mix(i, t)
            order(i, more, slot, lambda n, tk, s: task(i, n, tk, s))
        pairs(eng, body)

    m.engines = dict(sp=sp, pool=pool, pe=pe, dve=dve, act=act)
    m.after = [(out_made, B)]
    return m


def cross_attention_0(c):
    return cross_attention(c, 0)


def rows(buf):
    return lambda j: buf[:, j, :]


def feed_forward(c):
    m = Stage()
    k = Carver(c)
    oT, t, x2, t2 = k.f32(G, D), k.f32(G, D), k.f32(G, D), k.f32(G, D)
    x2T, hT = k.f32(G * P), k.f32(F0 // P, G * P)
    ln2, ln3 = Norm(c, k, "ff_ln2", ("ln2_g", "ln2_b")), Norm(c, k, "ff_ln3", ("ln3_g", "ln3_b"))
    turn = Turn(c, "ff_xT")
    s = {n: c.sem(f"ff_{n}") for n in ("o_copied", "proj", "added", "biased", "hidden_psum", "hidden", "out_psum",
                                       "summed", "summed_biased", "x_ready")}
    A_, B_ = (lambda j: c.ps[:, 2 * j, 0:P]), (lambda j: c.ps[:, 2 * j + 1, 0:P])
    Y_ = lambda j: c.ps[:, 4 + j, 0:P]

    def pe(eng):
        with eng.Fori(0, GROUPS) as g:
            eng.wait_ge(s["x_ready"], g * G)
            for j in range(G):
                eng.wait_ge(s["o_copied"], nth(g, j))
                eng.matmul(A_(j), oT[:, j, :], c.W("c_out"), start=True, stop=True).then_inc(s["proj"], 1)
            turn.pe(eng, g, rows(x2), B_, ln2.ready)
            eng.wait_ge(turn.ready, g * G + G)
            for f in range(F0 // P):
                eng.matmul(c.ps[:, f, :], c.W("ffn1", f * P, (f + 1) * P), x2T, start=True,
                           stop=True).then_inc(s["hidden_psum"], 1)
            eng.wait_ge(s["hidden"], (g + 1) * (F0 // P))
            for j in range(G):
                for f in range(F0 // P):
                    mm = eng.matmul(Y_(j), hT[:, f, j * P:(j + 1) * P], c.W("ffn2", f * D, (f + 1) * D),
                                    start=f == 0, stop=f == F0 // P - 1)
                mm.then_inc(s["out_psum"], 1)

    def act(eng):
        with eng.Fori(0, GROUPS) as g:
            eng.wait_ge(s["x_ready"], g * G)
            for j in range(G):
                eng.activation(oT[:, j, :], c.o[:, g * G + j, :], ACT.Copy).then_inc(s["o_copied"], 1)
            ln2.act(eng, g)
            turn.act(eng, g, B_, lambda j: x2T[:, j * P:(j + 1) * P])
            for f in range(F0 // P):
                eng.wait_ge(s["hidden_psum"], g * (F0 // P) + f + 1)
                eng.activation(hT[:, f, :], c.ps[:, f, :], ACT.Gelu, bias=c.W("ffn_b1", f, f + 1)).then_inc(s["hidden"], 1)
            ln3.act(eng, g)

    def dve(eng):
        with eng.Fori(0, GROUPS) as g:
            for j in range(G):
                eng.wait_ge(s["proj"], nth(g, j))
                eng.tensor_tensor(t[:, j, :], A_(j), c.y[:, g * G + j, :], ALU.add).then_inc(s["added"], 1)
            for j in range(G):
                eng.wait_ge(s["added"], nth(g, j))
                eng.tensor_tensor(t[:, j, :], t[:, j, :], c.R("c_out_b"), ALU.add).then_inc(s["biased"], 1)
            ln2.dve(eng, g, rows(t), rows(x2), wait=lambda j: eng.wait_ge(s["biased"], nth(g, j)))
            for j in range(G):
                eng.wait_ge(s["out_psum"], nth(g, j))
                eng.tensor_tensor(t2[:, j, :], Y_(j), x2[:, j, :], ALU.add).then_inc(s["summed"], 1)
            for j in range(G):
                eng.wait_ge(s["summed"], nth(g, j))
                eng.tensor_tensor(t2[:, j, :], t2[:, j, :], c.R("ffn_b2"), ALU.add).then_inc(s["summed_biased"], 1)
            ln3.dve(eng, g, rows(t2), rows(t), wait=lambda j: eng.wait_ge(s["summed_biased"], nth(g, j)))
            for j in range(G):
                eng.wait_ge(ln3.ready, nth(g, j))
                x = c.x[:, g * G + j, :]
                eng.tensor_tensor(x, x, t[:, j, :], ALU.add).then_inc(s["x_ready"], 1)

    m.engines = dict(pe=pe, dve=dve, act=act)
    m.after = [(s["x_ready"], PAIRS)]
    return m


def linear_attention(c):
    m = Stage()
    k = Carver(c)
    wq, wk, nb = k.f32(D), k.f32(D), k.f32(2)
    xn, xT = k.f32(G, D), k.f32(G, D)
    qf, kf, v = k.f32(G, 2, P), k.f32(G, 2, P), k.f32(G, D)
    qs = k.f32(G, 2, 2, LH * L)
    at = k.f32(G, LH * L)
    sq, on, oT = k.f32(G, D), k.f32(G, D), k.f32(G, D)
    ss, lg, rr = k.f32(G, LH), k.f32(G, LH), k.f32(G, LH)
    pre, turn, turno = Norm(c, k, "la_pre"), Turn(c, "la_xT"), Turn(c, "la_oT")
    s = {n: c.sem(f"la_{n}") for n in ("fold_psum", "folded", "proj", "features", "spread", "attn_psum", "attn", "mix",
                                       "squares", "sums", "logs", "rstd", "scaled", "heads", "out_psum", "x_ready")}
    A_, B_ = (lambda j: c.ps[:, 2 * j, 0:P]), (lambda j: c.ps[:, 2 * j + 1, 0:P])

    def pe(eng):
        eng.matmul(c.ps[:, 0, 0:D], c.W("l_wq"), c.W("l_fq"), start=True, stop=True)
        eng.matmul(c.ps[:, 0, D:2 * D], c.W("l_wk"), c.W("l_fk"), start=True, stop=True).then_inc(s["fold_psum"], 1)
        eng.wait_ge(s["folded"], 4)
        with eng.Fori(0, GROUPS) as g:
            eng.wait_ge(s["x_ready"], g * G)
            turn.pe(eng, g, rows(xn), A_, pre.ready)
            for j in range(G):
                eng.wait_ge(turn.ready, nth(g, j))
                eng.matmul(c.ps[:, 2 * j + 1, 0:P], wq, xT[:, j, :], start=True, stop=True)
                eng.matmul(c.ps[:, 2 * j + 1, P:2 * P], wk, xT[:, j, :], start=True, stop=True)
                eng.matmul(c.ps[:, 2 * j + 1, 2 * P:3 * P], xT[:, j, :], c.W("l_wv"), start=True,
                           stop=True).then_inc(s["proj"], 1)
            for j in range(G):
                eng.wait_ge(s["spread"], g * 4 * G + 4 * j + 4)
                eng.wait_ge(s["features"], g * 5 * G + 5 * j + 5)
                for b in range(2):
                    for f in range(2):
                        mm = eng.matmul(c.ps[b * L:(b + 1) * L, 2 * j, :], kf[:, j, f, b * L:(b + 1) * L],
                                        qs[:, j, f, b, :], start=f == 0, stop=f == 1)
                mm.then_inc(s["attn_psum"], 1)
            for j in range(G):
                eng.wait_ge(s["attn"], nth(g, j))
                eng.matmul(c.ps[:, 2 * j + 1, 511:512], c.C("ident"), c.C("ident")[:, 0:1], start=True, stop=True)
                for b in range(2):
                    r = slice(b * L, (b + 1) * L)
                    for h in range(LH):
                        mm = eng.matmul(c.ps[r, 2 * j + 1, h * LD:(h + 1) * LD], at[r, j, h * L:(h + 1) * L],
                                        v[r, j, h * LD:(h + 1) * LD], start=True, stop=True)
                mm.then_inc(s["mix"], 1)
            turno.pe(eng, g, rows(on), A_, s["heads"])
            for j in range(G):
                eng.wait_ge(turno.ready, nth(g, j))
                eng.matmul(B_(j), oT[:, j, :], c.W("l_wo"), start=True, stop=True).then_inc(s["out_psum"], 1)

    def act(eng):
        eng.wait_ge(s["fold_psum"], 1)
        eng.activation(wq, c.ps[:, 0, 0:D], ACT.Copy).then_inc(s["folded"], 1)
        eng.activation(wk, c.ps[:, 0, D:2 * D], ACT.Copy).then_inc(s["folded"], 1)
        eng.activation(nb[:, 0:1], c.W("l_bq"), ACT.Copy, scale=-1.0).then_inc(s["folded"], 1)
        eng.activation(nb[:, 1:2], c.W("l_bk"), ACT.Copy, scale=-1.0).then_inc(s["folded"], 1)
        eng.wait_ge(s["folded"], 4)
        with eng.Fori(0, GROUPS) as g:
            pre.act(eng, g)
            turn.act(eng, g, A_, rows(xT))
            for j in range(G):
                eng.wait_ge(s["proj"], nth(g, j))
                for dst, at_, b in ((qf, 0, "l_bq"), (kf, P, "l_bk")):
                    src = c.ps[:, 2 * j + 1, at_:at_ + P]
                    eng.activation(dst[:, j, 0, :], src, ACT.Exp, bias=c.W(b)).then_inc(s["features"], 1)
                    eng.activation(dst[:, j, 1, :], src, ACT.Exp, scale=-1.0,
                                   bias=nb[:, 0:1] if b == "l_bq" else nb[:, 1:2]).then_inc(s["features"], 1)
                eng.activation(v[:, j, :], c.ps[:, 2 * j + 1, 2 * P:3 * P], ACT.Copy).then_inc(s["features"], 1)
            for j in range(G):
                eng.wait_ge(s["mix"], nth(g, j))
                eng.activation(sq[:, j, :], B_(j), ACT.Square).then_inc(s["squares"], 1)
            eng.wait_ge(s["sums"], g * G + G)
            eng.activation(lg, ss, ACT.Ln, scale=1.0 / LD, bias=c.eps[:, 0:1]).then_inc(s["logs"], 1)
            eng.wait_ge(s["logs"], g + 1)
            eng.activation(rr, lg, ACT.Exp, scale=-0.5).then_inc(s["rstd"], 1)
            turno.act(eng, g, A_, rows(oT))

    def pool(eng):
        with eng.Fori(0, GROUPS) as g:
            for j in range(G):
                for f in range(2):
                    eng.wait_ge(s["features"], g * 5 * G + 5 * j + 1 + f)
                    for b in range(2):
                        eng.tensor_tensor(qs[:, j, f, b, :].rearrange("p (h q) -> p h q", h=LH),
                                          spread(qf[:, j, f, b * L:(b + 1) * L], LH, 1), spread(c.C("head16"), L),
                                          ALU.mult).then_inc(s["spread"], 1)

    def dve(eng):
        with eng.Fori(0, GROUPS) as g:
            pre.dve(eng, g, lambda j: c.x[:, g * G + j, :], rows(xn))
            for j in range(G):
                eng.wait_ge(s["attn_psum"], nth(g, j))
                eng.tensor_tensor(at[:, j, :].rearrange("p (h q) -> p h q", h=LH),
                                  c.ps[:, 2 * j, :].rearrange("p (h q) -> p h q", h=LH),
                                  spread(c.C("causal"), LH, 1), ALU.mult).then_inc(s["attn"], 1)
            for j in range(G):
                eng.wait_ge(s["squares"], nth(g, j))
                eng.tensor_reduce(ss[:, j, :], heads(sq[:, j, :], LH), AX, ALU.add).then_inc(s["sums"], 1)
            eng.wait_ge(s["rstd"], g + 1)
            for j in range(G):
                eng.tensor_tensor(heads(on[:, j, :], LH), heads(B_(j), LH), spread(rr[:, j, :], LD),
                                  ALU.mult).then_inc(s["scaled"], 1)
            for j in range(G):
                eng.wait_ge(s["scaled"], nth(g, j))
                eng.tensor_tensor(on[:, j, :], on[:, j, :], c.R("rms"), ALU.mult).then_inc(s["heads"], 1)
            for j in range(G):
                eng.wait_ge(s["out_psum"], nth(g, j))
                x = c.x[:, g * G + j, :]
                eng.tensor_tensor(x, B_(j), x, ALU.add).then_inc(s["x_ready"], 1)

    m.engines = dict(pe=pe, dve=dve, act=act, pool=pool)
    m.after = [(s["x_ready"], PAIRS)]
    return m


def mixture(c, layer):
    m = Stage()
    nm = f"m{layer}"
    k = Carver(c)
    if layer == 1:
        w1, w2 = k.f32(E * F1), k.f32(U1 * D)
        units, bias, router, row = U1, "m1_b1", "r1", "br1"
    else:
        w1, w2, w3 = k.f32(E * F2), k.f32(E * F2), k.f32(E * FT * D)
        units, bias, router, row = E * FT, "m2_b1", "r2", "br2"
    xn, xT = k.f32(G, D), k.f32(G * P)
    lg, nm_, ex, sm, rs = k.f32(G, E), k.f32(G, 1), k.f32(G, E), k.f32(G, 1), k.f32(G, 1)
    NS = 6
    pr, rest, m8 = k.f32(G, E + NS), k.f32(G, E + NS), k.f32(G, 8)
    comb, combT = k.f32(G, E), k.f32(G, P)
    NH = 4
    hT = k.f32(NH, G * P)
    gate = k.f32(2, G * P) if layer == 2 else None
    acc = k.f32(G, D)
    pre, turn = Norm(c, k, f"{nm}_pre"), Turn(c, f"{nm}_xT")
    names = ["w_loaded", "sentinels", "logits", "biased", "max", "exps", "recips", "probs", "top8", "marked", "chosen",
             "comb", "combT_psum", "combT", "bias_psum", "acc", "out_psum", "x_ready", "gate"]
    s = {n: c.sem(f"{nm}_{n}") for n in names}
    hp = [c.sem(f"{nm}_hidden_psum{i}") for i in range(2)]
    hr = [c.sem(f"{nm}_hidden{i}") for i in range(NH)]
    A = c.A
    nw = 2 if layer == 1 else 3

    def parts(e):
        if layer == 2:
            return [(e * FT + f, 0, P) for f in range(FT)]
        a = e * F1
        return [(a // P, 0, P), (a // P + 1, 0, P // 2)] if a % P == 0 else [(a // P, P // 2, P // 2), (a // P + 1, 0, P)]

    def sp(eng):
        eng.dma_start(w1, A[f"{nm}w1"]).then_inc(s["w_loaded"], 16)
        eng.dma_start(w2, A[f"{nm}w2"]).then_inc(s["w_loaded"], 16)
        if layer == 2:
            eng.dma_start(w3, A["m2w3"]).then_inc(s["w_loaded"], 16)

    LG = lambda j: c.ps[:, 1, j * E:(j + 1) * E]
    CT = lambda j: c.ps[0:E, 2, j * P:(j + 1) * P]
    BI = lambda j: c.ps[:, 3, j * P:(j + 1) * P]
    uses = [[u for u in range(units) if u % NH == q] for q in range(NH)]
    last_use = {}
    first_use = {}
    for e in range(E):
        for u, _, _ in parts(e):
            last_use[u] = e
            first_use.setdefault(u, e)

    def pe(eng):
        eng.wait_ge(s["w_loaded"], 16 * nw)
        with eng.Fori(0, GROUPS) as g:
            eng.wait_ge(s["x_ready"], g * G)
            turn.pe(eng, g, rows(xn), lambda j: c.ps[:, 4 + j, 0:P], pre.ready)
            eng.wait_ge(turn.ready, g * G + G)
            for j in range(G):
                mm = eng.matmul(LG(j), xT[:, j * P:(j + 1) * P], c.W(router), start=True, stop=True)
            mm.then_inc(s["logits"], 1)
            for j in range(G):
                eng.wait_ge(s["comb"], nth(g, j))
                mm = eng.transpose(CT(j), comb[:, j, :], c.C("ident"))
            mm.then_inc(s["combT_psum"], 1)
            eng.wait_ge(s["combT"], g + 1)
            for j in range(G):
                mm = eng.matmul(BI(j), combT[0:E, j, :], c.W("m1_b2" if layer == 1 else "m2_b3")[0:E, :], start=True, stop=True)
            mm.then_inc(s["bias_psum"], 1)
            eng.wait_ge(s["acc"], g * (E + 1) * G + G)

            def hidden(u):
                w = slice(u * P, (u + 1) * P)
                if layer == 1:
                    bk = u % 2
                    eng.wait_ge(hr[(u - 2) % NH], prev_count(g, u, 2))
                    eng.matmul(c.ps[:, bk, :], w1[:, w], xT, start=True, stop=True).then_inc(hp[bk], 1)
                else:
                    bk = 2 * (u % 2)
                    eng.wait_ge(hr[(u - 2) % NH], prev_count(g, u, 2))
                    eng.matmul(c.ps[:, bk, :], w1[:, w], xT, start=True, stop=True)
                    eng.matmul(c.ps[:, bk + 1, :], w2[:, w], xT, start=True, stop=True).then_inc(hp[u % 2], 1)

            def prev_count(g, u, back):
                v = u - back
                per = len(uses[v % NH])
                return g * per + v // NH + 1 if v >= 0 else g * per

            done = 0
            for e in range(E):
                need = max(u for u, _, _ in parts(e))
                while done <= min(need + 1, units - 1):
                    hidden(done)
                    done += 1
                for u, _, _ in parts(e):
                    eng.wait_ge(hr[u % NH], g * len(uses[u % NH]) + u // NH + 1)
                if e >= 2:
                    eng.wait_ge(s["acc"], g * (E + 1) * G + G * (e - 1) + G)
                ps = parts(e)
                for j in range(G):
                    for n, (u, r0, nr) in enumerate(ps):
                        wo = w2 if layer == 1 else w3
                        mm = eng.matmul(c.ps[:, 4 + e % 2, j * P:(j + 1) * P], hT[r0:r0 + nr, u % NH, j * P:(j + 1) * P],
                                        wo[r0:r0 + nr, u * D:(u + 1) * D], start=n == 0, stop=n == len(ps) - 1)
                mm.then_inc(s["out_psum"], 1)

    def free_hidden(eng, g, u):
        v = u - NH
        if v >= 0:
            eng.wait_ge(s["out_psum"], g * E + last_use[v] + 1)
        else:
            eng.wait_ge(s["out_psum"], g * E)

    def act(eng):
        with eng.Fori(0, GROUPS) as g:
            pre.act(eng, g)
            turn.act(eng, g, lambda j: c.ps[:, 4 + j, 0:P], lambda j: xT[:, j * P:(j + 1) * P])
            for j in range(G):
                eng.wait_ge(s["max"], nth(g, j))
                eng.activation(ex[:, j, :], lg[:, j, :], ACT.Exp, bias=nm_[:, j, :],
                               accum_out=sm[:, j, :]).then_inc(s["exps"], 1)
            eng.wait_ge(s["combT_psum"], g + 1)
            eng.activation(combT[0:E, :, :], c.ps[0:E, 2, :].rearrange("p (j n) -> p j n", j=G), ACT.Copy).then_inc(s["combT"], 1)
            for u in range(units):
                per2 = units // 2
                eng.wait_ge(hp[u % 2], g * per2 + u // 2 + 1)
                if layer == 1:
                    free_hidden(eng, g, u)
                    eng.activation(hT[:, u % NH, :], c.ps[:, u % 2, :], ACT.Gelu,
                                   bias=c.W(bias, u, u + 1)).then_inc(hr[u % NH], 1)
                else:
                    if u >= 2:
                        eng.wait_ge(hr[(u - 2) % NH], g * len(uses[0]) + (u - 2) // NH + 1)
                    eng.activation(gate[:, u % 2, :], c.ps[:, 2 * (u % 2), :], ACT.Silu,
                                   bias=c.W(bias, u, u + 1)).then_inc(s["gate"], 1)

    def dve(eng):
        eng.memset(pr[:, :, E:E + NS], BIG).then_inc(s["sentinels"], 1)
        with eng.Fori(0, GROUPS) as g:
            pre.dve(eng, g, lambda j: c.x[:, g * G + j, :], rows(xn))
            eng.wait_ge(s["logits"], g + 1)
            for j in range(G):
                eng.tensor_tensor(lg[:, j, :], LG(j), c.R(row), ALU.add).then_inc(s["biased"], 1)
            for j in range(G):
                eng.wait_ge(s["biased"], nth(g, j))
                eng.tensor_reduce(nm_[:, j, :], lg[:, j, :], AX, ALU.max, negate=True).then_inc(s["max"], 1)
            if layer == 1:
                for j in range(G):
                    eng.wait_ge(s["exps"], nth(g, j))
                    eng.reciprocal(rs[:, j, :], sm[:, j, :]).then_inc(s["recips"], 1)
                for j in range(G):
                    eng.wait_ge(s["recips"], nth(g, j))
                    eng.tensor_scalar(pr[:, j, 0:E], ex[:, j, :], rs[:, j, :], None, ALU.mult).then_inc(s["probs"], 1)
            else:
                for j in range(G):
                    eng.tensor_copy(pr[:, j, 0:E], lg[:, j, :]).then_inc(s["probs"], 1)
            for j in range(G):
                eng.wait_ge(s["sentinels"], 1)
                eng.wait_ge(s["probs"], nth(g, j))
                settle(c, eng)
                eng.max(m8[:, j, :], pr[:, j, :]).then_inc(s["top8"], 1)
            for j in range(G):
                eng.wait_ge(s["top8"], nth(g, j))
                settle(c, eng)
                eng.match_replace(rest[:, j, :], m8[:, j, :], pr[:, j, :], GONE).then_inc(s["marked"], 1)
            if layer == 1:
                for j in range(G):
                    eng.wait_ge(s["marked"], nth(g, j))
                    eng.scalar_tensor_tensor(out=comb[:, j, :], in0=rest[:, j, 0:E], scalar=GONE / 2, in1=pr[:, j, 0:E],
                                             op0=ALU.is_le, op1=ALU.mult).then_inc(s["comb"], 1)
            else:
                for j in range(G):
                    eng.wait_ge(s["marked"], nth(g, j))
                    eng.wait_ge(s["exps"], nth(g, j))
                    eng.scalar_tensor_tensor(out=ex[:, j, :], in0=rest[:, j, 0:E], scalar=GONE / 2, in1=ex[:, j, :],
                                             op0=ALU.is_le, op1=ALU.mult).then_inc(s["chosen"], 1)
                for j in range(G):
                    eng.wait_ge(s["chosen"], nth(g, j))
                    eng.tensor_reduce(rs[:, j, :], ex[:, j, :], AX, ALU.add).then_inc(s["recips"], 1)
                for j in range(G):
                    eng.wait_ge(s["recips"], g * 2 * G + j + 1)
                    eng.reciprocal(sm[:, j, :], rs[:, j, :]).then_inc(s["recips"], 1)
                for j in range(G):
                    eng.wait_ge(s["recips"], g * 2 * G + G + j + 1)
                    eng.tensor_scalar(comb[:, j, :], ex[:, j, :], sm[:, j, :], None, ALU.mult).then_inc(s["comb"], 1)
            eng.wait_ge(s["bias_psum"], g + 1)
            for j in range(G):
                eng.tensor_tensor(acc[:, j, :], BI(j), c.x[:, g * G + j, :], ALU.add).then_inc(s["acc"], 1)

            def results(e):
                eng.wait_ge(s["out_psum"], g * E + e + 1)
                for j in range(G):
                    eng.wait_ge(s["acc"], g * (E + 1) * G + e * G + j + 1)
                    eng.scalar_tensor_tensor(out=acc[:, j, :], in0=c.ps[:, 4 + e % 2, j * P:(j + 1) * P],
                                             scalar=comb[:, j, e:e + 1], in1=acc[:, j, :], op0=ALU.mult,
                                             op1=ALU.add).then_inc(s["acc"], 1)

            if layer == 2:
                for u in range(units):
                    if u % FT == 2 and u // FT >= 1:
                        results(u // FT - 1)
                    eng.wait_ge(s["gate"], g * units + u + 1)
                    free_hidden(eng, g, u)
                    eng.scalar_tensor_tensor(out=hT[:, u % NH, :], in0=c.ps[:, 2 * (u % 2) + 1, :],
                                             scalar=c.W("m2_b2", u, u + 1), in1=gate[:, u % 2, :], op0=ALU.add,
                                             op1=ALU.mult).then_inc(hr[u % NH], 1)
                results(E - 1)
            else:
                for e in range(E):
                    results(e)
            for j in range(G):
                eng.wait_ge(s["acc"], g * (E + 1) * G + E * G + j + 1)
                eng.tensor_scalar(c.x[:, g * G + j, :], acc[:, j, :], 1.0, None, ALU.mult).then_inc(s["x_ready"], 1)

    m.engines = dict(sp=sp, pe=pe, dve=dve, act=act)
    m.after = [(s["x_ready"], PAIRS)]
    return m


def mixture_0(c):
    return mixture(c, 1)


def queries_1(c):
    m = Stage()
    k = Carver(c)
    w = k.f32(4, HP * D)
    xn = k.f32(G, D)
    pre, turn = Norm(c, k, "q1_pre"), Turn(c, "q1_xT")
    s = {n: c.sem(f"q1_{n}") for n in ("w_loaded", "fold_psum", "folded")}

    def sp(eng):
        eng.dma_start(w.rearrange("p a n -> p (a n)"), c.A["xw"]).then_inc(s["w_loaded"], 16)

    def pe(eng):
        eng.wait_ge(s["w_loaded"], 16)
        for a in range(2):
            if a == 1:
                eng.wait_ge(s["folded"], 4)
            for q in range(4):
                for h2 in range(2):
                    r = slice(h2 * XD, (h2 + 1) * XD)
                    for x in range(2):
                        hp = 2 * q + x
                        mm = eng.matmul(c.ps[:, 2 * q + h2, x * D:(x + 1) * D], w[r, 2 * a, hp * D:(hp + 1) * D],
                                        w[r, 2 * a + 1, hp * D:(hp + 1) * D], start=True, stop=True)
                mm.then_inc(s["fold_psum"], 1)
        eng.wait_ge(s["folded"], 8)
        with eng.Fori(0, GROUPS) as g:
            turn.pe(eng, g, rows(xn), lambda j: c.ps[:, 2 * j, 0:P], pre.ready)

    def act(eng):
        for a, dst in ((0, c.fold), (1, c.foldv)):
            for q in range(4):
                eng.wait_ge(s["fold_psum"], 4 * a + q + 1)
                eng.activation(dst[:, 4 * q:4 * q + 4, :].rearrange("p (x h) d -> p h x d", h=2),
                               c.ps[:, 2 * q:2 * q + 2, 0:2 * D].rearrange("p h (x d) -> p h x d", x=2),
                               ACT.Copy).then_inc(s["folded"], 1)
        with eng.Fori(0, GROUPS) as g:
            pre.act(eng, g)
            turn.act(eng, g, lambda j: c.ps[:, 2 * j, 0:P], lambda j: c.xT[:, g * G + j, :])

    def dve(eng):
        with eng.Fori(0, GROUPS) as g:
            pre.dve(eng, g, lambda j: c.x[:, g * G + j, :], rows(xn), wait=lambda j: eng.wait_ge(turn.ready, g * G))

    m.engines = dict(sp=sp, pe=pe, dve=dve, act=act)
    m.after = [(turn.ready, PAIRS), (s["folded"], 8)]
    return m


def cross_attention_1(c):
    return cross_attention(c, 1)


def rotary_attention(c):
    m = Stage()
    k = Carver(c)
    wqr, wkr, br = k.f32(D), k.f32(D), k.f32(2)
    xn, xT = k.f32(G, D), k.f32(G, D)
    qT, kT, ta, tb = k.f32(G, D), k.f32(G, D), k.f32(G, 2, D), k.f32(G, 2, D)
    xm, dk, gz = k.f32(G, D), k.f32(G, H), k.f32(G, D)
    sc, dd = k.f32(G, H * L), k.f32(G, H * L)
    mx, den, rden = k.f32(G, H), k.f32(G, H), k.f32(G, H)
    on, oT, ge = k.f32(G, D), k.f32(G, D), k.f32(G, D)
    rs, ms = k.f32(G, H), k.f32(G, H)
    pre, turn, turno = Norm(c, k, "ra_pre"), Turn(c, "ra_xT"), Turn(c, "ra_oT")
    mix = HeadMix(c, k, "ra")
    s = {n: c.sem(f"ra_{n}") for n in (
        "x_biased", "rot_psum", "rot", "proj", "rot_a", "rot_b", "qk", "mean_psum", "mean", "decay_psum", "decay_z",
        "decay_e", "decay_e1", "decay_p", "decay_x", "decay", "dist", "scaled", "max", "shifted", "exps", "sums", "recips",
        "heads", "attn", "gate_psum", "gate_z", "gate_e", "gate_e1", "gate_r", "gate", "rowsum", "mu_psum", "centred",
        "sqs", "sqsum", "var_psum", "logs", "rstd", "normed", "g1", "g2", "gated", "out_psum", "x_ready")}
    A_, B_ = (lambda j: c.ps[:, 2 * j, 0:P]), (lambda j: c.ps[:, 2 * j + 1, 0:P])
    PQ = lambda j, n: c.ps[:, 2 * j, n * P:(n + 1) * P]

    def steps(eng, sems, g, fn):
        for j in range(G):
            for q in sems:
                eng.wait_ge(s[q] if isinstance(q, str) else q, nth(g, j))
            fn(j)

    def pe(eng):
        for n, (w, b) in enumerate((("a_wq", "a_bq"), ("a_wk", "a_bk"))):
            eng.matmul(c.ps[:, 0, n * D:(n + 1) * D], c.W(w), c.C("rot"), start=True, stop=True)
            mm = eng.matmul(c.ps[:, 0, 2 * D + n:2 * D + n + 1], c.C("rot"), c.W(b), start=True, stop=True)
        mm.then_inc(s["rot_psum"], 1)
        eng.wait_ge(s["rot"], 3)
        with eng.Fori(0, GROUPS) as g:
            eng.wait_ge(s["x_ready"], g * G)
            turn.pe(eng, g, rows(xn), B_, pre.ready)
            def project(j):
                for n, w in enumerate((c.W("a_wqT"), wqr, c.W("a_wkT"), wkr)):
                    mm = eng.matmul(PQ(j, n), w, xT[:, j, :], start=True, stop=True)
                mm.then_inc(s["proj"], 1)
            steps(eng, [turn.ready], g, project)
            steps(eng, [turn.ready], g, lambda j: eng.matmul(B_(j), xn[:, j, :], c.C("avg64"), start=True,
                                                             stop=True).then_inc(s["mean_psum"], 1))
            def decay(j):
                eng.matmul(c.ps[:, 2 * j + 1, P:P + H], xm[:, j, :], c.W("a_wd"), start=True, stop=True)
                eng.matmul(c.ps[:, 2 * j + 1, 2 * P:3 * P], xT[:, j, :], c.W("a_wg"), start=True,
                           stop=True).then_inc(s["decay_psum"], 1)
            steps(eng, ["mean"], g, decay)
            for j in range(G):
                eng.wait_ge(s["decay_z"], nth(g, j))
                eng.wait_ge(s["gate_z"], nth(g, j))
            mix.pe_values(eng, g, rows(xT), turn.ready, c.W("a_wv"))
            for j in range(G):
                eng.wait_ge(s["rot_a"], g * 2 * G + 2 * j + 2)
                eng.wait_ge(s["rot_b"], g * 2 * G + 2 * j + 2)
            mix.pe_scores(eng, g, rows(qT), s["qk"], None)
            mix.pe_turn(eng, g, rows(sc), s["exps"], s["scaled"])
            mix.pe_mix(eng, g)
            steps(eng, ["rowsum"], g, lambda j: eng.matmul(c.ps[:, 2 * j + 1, 0:H], c.C("avg512"), rs[:, j, :], start=True,
                                                           stop=True).then_inc(s["mu_psum"], 1))
            steps(eng, ["sqsum", "centred"], g, lambda j: eng.matmul(c.ps[:, 2 * j + 1, 0:H], c.C("avg512"), ms[:, j, :],
                                                          start=True, stop=True).then_inc(s["var_psum"], 1))
            turno.pe(eng, g, rows(on), A_, s["gated"])
            steps(eng, [turno.ready], g, lambda j: eng.matmul(B_(j), oT[:, j, :], c.W("a_wo"), start=True,
                                                              stop=True).then_inc(s["out_psum"], 1))

    def act(eng):
        eng.wait_ge(s["rot_psum"], 1)
        eng.activation(wqr, c.ps[:, 0, 0:D], ACT.Copy).then_inc(s["rot"], 1)
        eng.activation(wkr, c.ps[:, 0, D:2 * D], ACT.Copy).then_inc(s["rot"], 1)
        eng.activation(br, c.ps[:, 0, 2 * D:2 * D + 2], ACT.Copy).then_inc(s["rot"], 1)
        with eng.Fori(0, GROUPS) as g:
            pre.act(eng, g)
            turn.act(eng, g, B_, rows(xT))
            steps(eng, ["mean_psum"], g, lambda j: eng.activation(xm[:, j, :], B_(j), ACT.Copy).then_inc(s["mean"], 1))
            steps(eng, ["decay_z"], g, lambda j: eng.activation(dk[:, j, :], dk[:, j, :], ACT.Exp,
                                                                scale=-1.0).then_inc(s["decay_e"], 1))
            steps(eng, ["gate_z"], g, lambda j: eng.activation(ge[:, j, :], gz[:, j, :], ACT.Exp,
                                                               scale=-1.0).then_inc(s["gate_e"], 1))
            steps(eng, ["decay_p"], g, lambda j: eng.activation(dk[:, j, :], dk[:, j, :], ACT.Exp, scale=-8.0 * LN2,
                                                                bias=c.dec[:, 0:1]).then_inc(s["decay_x"], 1))
            steps(eng, ["decay_x"], g, lambda j: eng.activation(dk[:, j, :], dk[:, j, :], ACT.Ln, scale=-1.0,
                                                                bias=c.one[:, 0:1]).then_inc(s["decay"], 1))
            steps(eng, ["shifted"], g, lambda j: eng.activation(sc[:, j, :], sc[:, j, :], ACT.Exp).then_inc(s["exps"], 1))
            mix.act_turn(eng, g)
            eng.wait_ge(s["var_psum"], g * G + G)
            for j in range(G):
                eng.activation(rs[:, j, :], c.ps[:, 2 * j + 1, 0:H], ACT.Ln, bias=c.eps[:, 0:1]).then_inc(s["logs"], 1)
            for j in range(G):
                eng.wait_ge(s["logs"], nth(g, j))
                eng.activation(rs[:, j, :], rs[:, j, :], ACT.Exp, scale=-0.5).then_inc(s["rstd"], 1)
            turno.act(eng, g, A_, rows(oT))

    def pool(eng):
        with eng.Fori(0, GROUPS) as g:
            mix.pool_spread(eng, g, rows(kT), s["qk"])
            def dist(j):
                for x in range(2):
                    eng.tensor_tensor(heads(dd[:, j, x * 512:(x + 1) * 512], LH), spread(c.C("dist"), LH, 1),
                                      spread(dk[:, j, x * LH:(x + 1) * LH], L), ALU.mult).then_inc(s["dist"], 1)
            steps(eng, ["decay"], g, dist)

    def dve(eng):
        with eng.Fori(0, GROUPS) as g:
            eng.wait_ge(turno.ready, g * G)
            pre.dve(eng, g, lambda j: c.x[:, g * G + j, :], rows(xn))
            def biased(j):
                x = c.x[:, g * G + j, :]
                eng.tensor_tensor(x, x, c.R("a_bo"), ALU.add).then_inc(s["x_biased"], 1)
            steps(eng, [pre.ready], g, biased)
            cs = lambda n: spread(c.C(n), 2, 1)
            two = lambda a: a.rearrange("p (b q) -> p b q", b=2)
            def rot_a(j):
                for n, b in enumerate(("a_bq", "a_bk")):
                    eng.scalar_tensor_tensor(out=two(ta[:, j, n, :]), in0=two(PQ(j, 2 * n)), scalar=c.W(b), in1=cs("cos"),
                                             op0=ALU.add, op1=ALU.mult).then_inc(s["rot_a"], 1)
                for n in range(2):
                    eng.scalar_tensor_tensor(out=two(tb[:, j, n, :]), in0=two(PQ(j, 2 * n + 1)), scalar=br[:, n:n + 1],
                                             in1=cs("sin"), op0=ALU.add, op1=ALU.mult).then_inc(s["rot_b"], 1)
            steps(eng, ["proj"], g, rot_a)
            for j in range(G):
                eng.wait_ge(s["rot_a"], g * 2 * G + 2 * j + 2)
                eng.wait_ge(s["rot_b"], g * 2 * G + 2 * j + 2)
                eng.tensor_tensor(qT[:, j, :], ta[:, j, 0, :], tb[:, j, 0, :], ALU.add)
                eng.tensor_tensor(kT[:, j, :], ta[:, j, 1, :], tb[:, j, 1, :], ALU.add).then_inc(s["qk"], 1)
            steps(eng, ["decay_psum"], g, lambda j: eng.tensor_tensor(dk[:, j, :], c.ps[:, 2 * j + 1, P:P + H], c.R("a_bd"),
                                                                      ALU.add).then_inc(s["decay_z"], 1))
            steps(eng, [], g, lambda j: eng.tensor_tensor(gz[:, j, :], c.ps[:, 2 * j + 1, 2 * P:3 * P], c.R("a_bg"),
                                                          ALU.add).then_inc(s["gate_z"], 1))
            mix.dve_values(eng, g)
            steps(eng, ["decay_e"], g, lambda j: eng.tensor_scalar(dk[:, j, :], dk[:, j, :], 1.0, None,
                                                                   ALU.add).then_inc(s["decay_e1"], 1))
            steps(eng, ["decay_e1"], g, lambda j: eng.reciprocal(dk[:, j, :], dk[:, j, :]).then_inc(s["decay_p"], 1))
            steps(eng, ["gate_e"], g, lambda j: eng.tensor_scalar(ge[:, j, :], ge[:, j, :], 1.0, None,
                                                                  ALU.add).then_inc(s["gate_e1"], 1))
            steps(eng, ["gate_e1"], g, lambda j: eng.reciprocal(ge[:, j, :], ge[:, j, :]).then_inc(s["gate_r"], 1))
            steps(eng, ["gate_r"], g, lambda j: eng.tensor_tensor(ge[:, j, :], ge[:, j, :], gz[:, j, :],
                                                                  ALU.mult).then_inc(s["gate"], 1))
            def scaled(j):
                eng.wait_ge(s["dist"], g * 2 * G + 2 * j + 2)
                eng.wait_ge(mix.s_scores, nth(g, j))
                eng.scalar_tensor_tensor(out=sc[:, j, :], in0=c.ps[:, 2 * j:2 * j + 2, :].rearrange("p x n -> p (x n)"),
                                         scalar=HD ** -0.5, in1=dd[:, j, :], op0=ALU.mult, op1=ALU.add).then_inc(s["scaled"], 1)
            steps(eng, [], g, scaled)
            steps(eng, ["scaled"], g, lambda j: eng.tensor_reduce(mx[:, j, :], heads(sc[:, j, :]), AX,
                                                                  ALU.max).then_inc(s["max"], 1))
            steps(eng, ["max"], g, lambda j: eng.tensor_tensor(heads(sc[:, j, :]), heads(sc[:, j, :]),
                                                               spread(mx[:, j, :], L), ALU.subtract).then_inc(s["shifted"], 1))
            steps(eng, ["exps"], g, lambda j: eng.tensor_reduce(den[:, j, :], heads(sc[:, j, :]), AX,
                                                                ALU.add).then_inc(s["sums"], 1))
            steps(eng, ["sums"], g, lambda j: eng.reciprocal(rden[:, j, :], den[:, j, :]).then_inc(s["recips"], 1))
            def attn(j):
                eng.wait_ge(mix.s_o, nth(g, j))
                eng.tensor_tensor(heads(on[:, j, :]), heads(A_(j)), spread(rden[:, j, :], HD),
                                  ALU.mult).then_inc(s["heads"], 1)
            steps(eng, ["recips"], g, attn)
            steps(eng, ["heads"], g, lambda j: eng.tensor_tensor(on[:, j, :], on[:, j, :], c.R("a_bv"),
                                                                 ALU.add).then_inc(s["attn"], 1))
            steps(eng, ["attn"], g, lambda j: eng.tensor_reduce(rs[:, j, :], heads(on[:, j, :]), AX,
                                                                ALU.add).then_inc(s["rowsum"], 1))
            steps(eng, ["mu_psum"], g, lambda j: eng.tensor_tensor(heads(on[:, j, :]), heads(on[:, j, :]),
                  spread(c.ps[:, 2 * j + 1, 0:H], HD), ALU.subtract).then_inc(s["centred"], 1))
            steps(eng, ["centred"], g, lambda j: eng.tensor_tensor(gz[:, j, :], on[:, j, :], on[:, j, :],
                                                                   ALU.mult).then_inc(s["sqs"], 1))
            steps(eng, ["sqs"], g, lambda j: eng.tensor_reduce(ms[:, j, :], heads(gz[:, j, :]), AX,
                                                               ALU.add).then_inc(s["sqsum"], 1))
            steps(eng, ["rstd"], g, lambda j: eng.tensor_tensor(heads(on[:, j, :]), heads(on[:, j, :]),
                  spread(rs[:, j, :], HD), ALU.mult).then_inc(s["normed"], 1))
            steps(eng, ["normed"], g, lambda j: eng.tensor_tensor(on[:, j, :], on[:, j, :], c.R("a_g"),
                                                                  ALU.mult).then_inc(s["g1"], 1))
            steps(eng, ["g1"], g, lambda j: eng.tensor_tensor(on[:, j, :], on[:, j, :], c.R("a_b"),
                                                              ALU.add).then_inc(s["g2"], 1))
            steps(eng, ["g2"], g, lambda j: eng.tensor_tensor(on[:, j, :], on[:, j, :], ge[:, j, :],
                                                              ALU.mult).then_inc(s["gated"], 1))
            def out(j):
                x = c.x[:, g * G + j, :]
                eng.tensor_tensor(x, B_(j), x, ALU.add).then_inc(s["x_ready"], 1)
            steps(eng, ["out_psum"], g, out)

    m.engines = dict(pe=pe, dve=dve, act=act, pool=pool)
    m.after = [(s["x_ready"], PAIRS)]
    return m


def mixture_1(c):
    return mixture(c, 2)


def residual_1(c):
    m = Stage()
    added, biased = c.sem("x_with_cross"), c.sem("x_with_cross_bias")

    def dve(eng):
        for h in range(2):
            r = slice(h * PAIRS // 2, (h + 1) * PAIRS // 2)
            eng.tensor_tensor(c.x[:, r, :], c.x[:, r, :], c.o[:, r, :], ALU.add).then_inc(added, 1)
        for h in range(2):
            r = slice(h * PAIRS // 2, (h + 1) * PAIRS // 2)
            eng.wait_ge(added, h + 1)
            eng.tensor_tensor(c.x[:, r, :], c.x[:, r, :], spread(c.R("x_b"), PAIRS // 2, 1), ALU.add).then_inc(biased, 1)

    m.engines = dict(dve=dve)
    m.after = [(biased, 2)]
    return m


_INS = ["x", "ctxT", "ctx", "mask", "weights", "rows", "consts", "m1w1", "m1w2", "m2w1", "m2w2", "m2w3", "xw"]


def kernel(**inputs):
    import numpy as _np
    import concourse.bacc as _bacc
    from concourse import mybir as _mybir
    from concourse.bass_utils import run_bass_kernel_spmd as _run

    v = {n: _np.asarray(a) for n, a in inputs.items()}
    f = _np.float32

    def rows_of(a, n=P):
        t = a.shape[0] // n
        return a.reshape(t, n, -1).transpose(1, 0, 2).reshape(n, -1)

    def col(a):
        return a.reshape(-1, 1) if a.shape[0] == P else _np.tile(a, P // a.shape[0]).reshape(-1, 1)

    def top(a):
        z = _np.zeros((P, a.shape[1]), f)
        z[:a.shape[0]] = a
        return z

    def blocks(a):
        z = _np.zeros((P, P), f)
        for i in range(LH):
            z[i * LD:(i + 1) * LD, i * LD:(i + 1) * LD] = a
        return z

    ciw, cib = v["L0_xattn_cross_in_w"], v["L0_xattn_cross_in_b"]
    w = dict(self_out=v["L0_xattn_self_out_w"].T, c_wq=ciw[:D], c_wk=ciw[D:2 * D], c_wv=ciw[2 * D:].T,
             c_out=v["L0_xattn_cross_out_w"].T, ffn1=v["L0_xattn_ffn_w1"].T, ffn2=rows_of(v["L0_xattn_ffn_w2"].T),
             l_wq=v["L0_attn_Wq"], l_wk=v["L0_attn_Wk"], l_wv=v["L0_attn_Wv"].T, l_wo=v["L0_attn_Wo"].T,
             l_fq=blocks(v["L0_attn_fmq_w"].T), l_fk=blocks(v["L0_attn_fmk_w"].T),
             r1=v["L0_ffn_Wr"], r2=v["L1_ffn_Wr"], m1_b1=rows_of(v["L0_ffn_b1"].reshape(-1, 1)),
             m1_b2=top(v["L0_ffn_b2"]), m2_b1=rows_of(v["L1_ffn_b1"].reshape(-1, 1)),
             m2_b2=rows_of(v["L1_ffn_b2"].reshape(-1, 1)), m2_b3=top(v["L1_ffn_b3"]),
             a_wq=v["L1_attn_wq"], a_wqT=v["L1_attn_wq"].T, a_wk=v["L1_attn_wk"], a_wkT=v["L1_attn_wk"].T,
             a_wv=v["L1_attn_wv"].T, a_wg=v["L1_attn_wg"].T, a_wo=v["L1_attn_wo"].T, a_wd=v["L1_attn_wd"].T,
             c_bq=col(cib[:D]), c_bv=col(cib[2 * D:]), ffn_b1=rows_of(v["L0_xattn_ffn_b1"].reshape(-1, 1)),
             l_bq=col(v["L0_attn_fmq_b"]), l_bk=col(v["L0_attn_fmk_b"]),
             a_bq=col(v["L1_attn_bq"]), a_bk=col(v["L1_attn_bk"]))
    r = dict(self_out_b="L0_xattn_self_out_b", c_out_b="L0_xattn_cross_out_b", ln1_g="L0_xattn_ln1_g",
             ln1_b="L0_xattn_ln1_b", ln2_g="L0_xattn_ln2_g", ln2_b="L0_xattn_ln2_b", ln3_g="L0_xattn_ln3_g",
             ln3_b="L0_xattn_ln3_b", ffn_b2="L0_xattn_ffn_b2", rms="L0_attn_rms_w", x_b="L1_xattn_b_out",
             a_bv="L1_attn_bv", a_bg="L1_attn_bg", a_bo="L1_attn_bo", a_g="L1_attn_gamma", a_b="L1_attn_beta",
             br1="L0_ffn_br", br2="L1_ffn_br", a_bd="L1_attn_bd")
    row = lambda a, n: _np.tile(a, n // a.shape[0])
    ctx = v["ctx_1024"]
    a = dict(
        x=v["x"], ctx=ctx, ctxT=_np.ascontiguousarray(ctx.transpose(0, 2, 1)),
        mask=v["mask_BxS2_bf1"].view(_np.uint8),
        weights=_np.concatenate([w[n].reshape(P, width) for n, width in W_ITEMS], 1),
        rows=_np.broadcast_to(_np.concatenate([row(v[r[n]], width) for n, width in R_ITEMS])[None], (P, R_N)),
        consts=constants(),
        m1w1=v["L0_ffn_W1"].transpose(1, 0, 2).reshape(P, E * F1), m1w2=rows_of(v["L0_ffn_W2"].reshape(E * F1, D)),
        m2w1=v["L1_ffn_W1"].transpose(1, 0, 2).reshape(P, E * F2), m2w2=v["L1_ffn_W2"].transpose(1, 0, 2).reshape(P, E * F2),
        m2w3=rows_of(v["L1_ffn_W3"].reshape(E * F2, D)),
        xw=_np.concatenate([rows_of(t) for t in (v["L1_xattn_Wq"], v["L1_xattn_Wkv"][:H * XD], v["L1_xattn_Wkv"][H * XD:],
                                                 v["L1_xattn_Wout"].T)], 1),
    )
    nc = _bacc.Bacc("TRN2", target_bir_lowering=False, num_devices=1)
    arrays, args = {}, {}
    for name in _INS:
        arr = _np.ascontiguousarray(a[name])
        arrays[f"in_{name}"] = arr
        args[name] = nc.dram_tensor(f"in_{name}", arr.shape, _mybir.dt.from_np(arr.dtype), kind="ExternalInput").ap()
    out = nc.dram_tensor("out_x", (B, L, D), F32, kind="ExternalOutput").ap()
    build(nc, args, out, STAGES)
    res = _run(nc, [arrays], core_ids=[0])
    return res.results[0]["out_x"]
```
